# Optimizing a Trainium2 kernel written in Bass

```python
import numpy as np
import jax
import jax.numpy as jnp

def _softmax(x, axis=-1):
    return jax.nn.softmax(x, axis=axis)

def _gelu(x):
    return jax.nn.gelu(x, approximate=True)

def _silu(x):
    return jax.nn.silu(x)

def _sigmoid(x):
    return jax.nn.sigmoid(x)

def _layernorm(x, axis=-1, eps=1e-05):
    m = jnp.mean(x, axis=axis, keepdims=True)
    v = jnp.var(x, axis=axis, keepdims=True)
    return (x - m) / jnp.sqrt(v + eps)

def _scatter_add(tgt, idx, src, axis=0):
    return tgt.at[idx].add(src)

def _segment_sum(src, seg, n):
    return jax.ops.segment_sum(src, seg, n)
kernel_name = 'mk_xattn_seq_d1_seqx_r4_ef9d15'

def setup_inputs(seed: int=0):
    np.random.seed(seed)
    _w = jnp.asarray

    def _rec_inputs():
        import jax
        import jax.numpy as jnp
        _rk = jax.random.key(seed)
        x = -0.0005207 + 1.001 * jax.random.normal(jax.random.fold_in(_rk, 1), (4, 512, 512), jnp.float32)
        _lenS = 512 - jax.random.randint(jax.random.fold_in(_rk, 7), (4,), 0, max(1, 512 // 4) + 1, jnp.int32)
        _lenS2 = 64 - jax.random.randint(jax.random.fold_in(_rk, 8), (4,), 0, max(1, 64 // 4) + 1, jnp.int32)
        _ctx_2048P = jax.random.normal(jax.random.fold_in(_rk, 11), (4, 16, 512), jnp.float32)
        _ctx_2048c = jax.random.dirichlet(jax.random.fold_in(_rk, 511), 0.3 * jnp.ones((16,), jnp.float32), (4, 64))
        _ctx_2048t = jnp.einsum('bsk,bkd->bsd', _ctx_2048c, _ctx_2048P)
        _ctx_2048t = _ctx_2048t * jax.lax.rsqrt(jnp.mean(jnp.square(_ctx_2048t)) + 1e-12) * 0.953939
        ctx_2048 = 2.81802e-05 + 1.00001 * (_ctx_2048t + 0.3 * jax.random.normal(jax.random.fold_in(_rk, 611), (4, 64, 512), jnp.float32))
        return (x, ctx_2048)
    x, ctx_2048 = _rec_inputs()

    def _L0_xattn_setup():
        import jax, jax.numpy as jnp
        import numpy as np
        B, Q, S1, S2 = (4, 64, 512, 512)
        D, H, K, F = (512, 16, 128, 2048)
        LN_EPS = 1e-05

        def _layer_norm(x, scale, offset):
            mu = jnp.mean(x, axis=-1, keepdims=True)
            var = jnp.var(x, axis=-1, keepdims=True)
            return (x - mu) * jax.lax.rsqrt(var + LN_EPS) * scale + offset

        def _cross_attention(q_in, kv_in, wq, bq, wk, bk, wv, bv, wo, bo, bias_k, bias_v):
            b, q_len, _ = q_in.shape
            t = kv_in.shape[1]
            qh = (q_in @ wq + bq).reshape(b, q_len, H, K)
            kh = (kv_in @ wk + bk).reshape(b, t, H, K)
            vh = (kv_in @ wv + bv).reshape(b, t, H, K)
            kh = jnp.concatenate([kh, jnp.broadcast_to(bias_k, (b, 1, H, K))], axis=1)
            vh = jnp.concatenate([vh, jnp.broadcast_to(bias_v, (b, 1, H, K))], axis=1)
            scale = jnp.sqrt(jnp.asarray(K, q_in.dtype))
            logits = jnp.einsum('bqhk,bthk->bhqt', qh, kh) / scale
            weights = jax.nn.softmax(logits, axis=-1)
            ctx = jnp.einsum('bhqt,bthk->bqhk', weights, vh).reshape(b, q_len, H * K)
            return ctx @ wo + bo

        def _forward(x, xf_1, xf_2, ln1_scale, ln1_offset, wq1, bq1, wk1, bk1, wv1, bv1, wo1, bo1, bias_k1, bias_v1, ln2_scale, ln2_offset, wq2, bq2, wk2, bk2, wv2, bv2, wo2, bo2, bias_k2, bias_v2, ln_mlp_scale, ln_mlp_offset, w_fc1, b_fc1, w_fc2, b_fc2):
            res = x
            h = _layer_norm(x, ln1_scale, ln1_offset)
            x = res + _cross_attention(h, xf_1, wq1, bq1, wk1, bk1, wv1, bv1, wo1, bo1, bias_k1, bias_v1)
            res = x
            h = _layer_norm(x, ln2_scale, ln2_offset)
            x = res + _cross_attention(h, xf_2, wq2, bq2, wk2, bk2, wv2, bv2, wo2, bo2, bias_k2, bias_v2)
            h = _layer_norm(x, ln_mlp_scale, ln_mlp_offset)
            h = jax.nn.gelu(h @ w_fc1 + b_fc1, approximate=False) @ w_fc2 + b_fc2
            return x + h
        key = jax.random.key(seed)
        ks = iter(jax.random.split(key, 64))

        def rn(shape, s=0.02):
            return jax.random.normal(next(ks), shape, jnp.float32) * s
        inp = {'x': rn((B, Q, D), 1.0), 'xf_1': rn((B, S1, D), 1.0), 'xf_2': rn((B, S2, D), 1.0)}
        for i in (1, 2):
            inp[f'ln{i}_scale'] = jnp.ones((D,), jnp.float32)
            inp[f'ln{i}_offset'] = jnp.zeros((D,), jnp.float32)
            inp[f'wq{i}'] = rn((D, H * K))
            inp[f'bq{i}'] = jnp.zeros((H * K,), jnp.float32)
            inp[f'wk{i}'] = rn((D, H * K))
            inp[f'bk{i}'] = jnp.zeros((H * K,), jnp.float32)
            inp[f'wv{i}'] = rn((D, H * K))
            inp[f'bv{i}'] = jnp.zeros((H * K,), jnp.float32)
            inp[f'wo{i}'] = rn((H * K, D))
            inp[f'bo{i}'] = jnp.zeros((D,), jnp.float32)
            inp[f'bias_k{i}'] = rn((1, 1, H, K))
            inp[f'bias_v{i}'] = rn((1, 1, H, K))
        inp['ln_mlp_scale'] = jnp.ones((D,), jnp.float32)
        inp['ln_mlp_offset'] = jnp.zeros((D,), jnp.float32)
        inp['w_fc1'] = rn((D, F))
        inp['b_fc1'] = jnp.zeros((F,), jnp.float32)
        inp['w_fc2'] = rn((F, D))
        inp['b_fc2'] = jnp.zeros((D,), jnp.float32)
        return inp
    _L0_xattn_all = _L0_xattn_setup()
    _L0_xattn_in = {k: v for k, v in _L0_xattn_all.items() if k in ('ln1_scale', 'ln1_offset', 'wq1', 'bq1', 'wk1', 'bk1', 'wv1', 'bv1', 'wo1', 'bo1', 'bias_k1', 'bias_v1', 'ln2_scale', 'ln2_offset', 'wq2', 'bq2', 'wk2', 'bk2', 'wv2', 'bv2', 'wo2', 'bo2', 'bias_k2', 'bias_v2', 'ln_mlp_scale', 'ln_mlp_offset', 'w_fc1', 'b_fc1', 'w_fc2', 'b_fc2')}
    del _L0_xattn_all
    return {'x': x, 'ctx_2048': ctx_2048, 'L0_xattn_ln1_scale': _L0_xattn_in['ln1_scale'], 'L0_xattn_ln1_offset': _L0_xattn_in['ln1_offset'], 'L0_xattn_wq1': _L0_xattn_in['wq1'], 'L0_xattn_bq1': _L0_xattn_in['bq1'], 'L0_xattn_wk1': _L0_xattn_in['wk1'], 'L0_xattn_bk1': _L0_xattn_in['bk1'], 'L0_xattn_wv1': _L0_xattn_in['wv1'], 'L0_xattn_bv1': _L0_xattn_in['bv1'], 'L0_xattn_wo1': _L0_xattn_in['wo1'], 'L0_xattn_bo1': _L0_xattn_in['bo1'], 'L0_xattn_bias_k1': _L0_xattn_in['bias_k1'], 'L0_xattn_bias_v1': _L0_xattn_in['bias_v1'], 'L0_xattn_ln2_scale': _L0_xattn_in['ln2_scale'], 'L0_xattn_ln2_offset': _L0_xattn_in['ln2_offset'], 'L0_xattn_wq2': _L0_xattn_in['wq2'], 'L0_xattn_bq2': _L0_xattn_in['bq2'], 'L0_xattn_wk2': _L0_xattn_in['wk2'], 'L0_xattn_bk2': _L0_xattn_in['bk2'], 'L0_xattn_wv2': _L0_xattn_in['wv2'], 'L0_xattn_bv2': _L0_xattn_in['bv2'], 'L0_xattn_wo2': _L0_xattn_in['wo2'], 'L0_xattn_bo2': _L0_xattn_in['bo2'], 'L0_xattn_bias_k2': _L0_xattn_in['bias_k2'], 'L0_xattn_bias_v2': _L0_xattn_in['bias_v2'], 'L0_xattn_ln_mlp_scale': _L0_xattn_in['ln_mlp_scale'], 'L0_xattn_ln_mlp_offset': _L0_xattn_in['ln_mlp_offset'], 'L0_xattn_w_fc1': _L0_xattn_in['w_fc1'], 'L0_xattn_b_fc1': _L0_xattn_in['b_fc1'], 'L0_xattn_w_fc2': _L0_xattn_in['w_fc2'], 'L0_xattn_b_fc2': _L0_xattn_in['b_fc2']}

def reference(x, ctx_2048, L0_xattn_ln1_scale, L0_xattn_ln1_offset, L0_xattn_wq1, L0_xattn_bq1, L0_xattn_wk1, L0_xattn_bk1, L0_xattn_wv1, L0_xattn_bv1, L0_xattn_wo1, L0_xattn_bo1, L0_xattn_bias_k1, L0_xattn_bias_v1, L0_xattn_ln2_scale, L0_xattn_ln2_offset, L0_xattn_wq2, L0_xattn_bq2, L0_xattn_wk2, L0_xattn_bk2, L0_xattn_wv2, L0_xattn_bv2, L0_xattn_wo2, L0_xattn_bo2, L0_xattn_bias_k2, L0_xattn_bias_v2, L0_xattn_ln_mlp_scale, L0_xattn_ln_mlp_offset, L0_xattn_w_fc1, L0_xattn_b_fc1, L0_xattn_w_fc2, L0_xattn_b_fc2):
    import jax
    import jax.numpy as jnp

    def _L0_xattn_ref(x, xf_1, xf_2, ln1_scale, ln1_offset, wq1, bq1, wk1, bk1, wv1, bv1, wo1, bo1, bias_k1, bias_v1, ln2_scale, ln2_offset, wq2, bq2, wk2, bk2, wv2, bv2, wo2, bo2, bias_k2, bias_v2, ln_mlp_scale, ln_mlp_offset, w_fc1, b_fc1, w_fc2, b_fc2):
        import jax, jax.numpy as jnp
        import numpy as np
        B, Q, S1, S2 = (4, 64, 512, 512)
        D, H, K, F = (512, 16, 128, 2048)
        LN_EPS = 1e-05

        def _layer_norm(x, scale, offset):
            mu = jnp.mean(x, axis=-1, keepdims=True)
            var = jnp.var(x, axis=-1, keepdims=True)
            return (x - mu) * jax.lax.rsqrt(var + LN_EPS) * scale + offset

        def _cross_attention(q_in, kv_in, wq, bq, wk, bk, wv, bv, wo, bo, bias_k, bias_v):
            b, q_len, _ = q_in.shape
            t = kv_in.shape[1]
            qh = (q_in @ wq + bq).reshape(b, q_len, H, K)
            kh = (kv_in @ wk + bk).reshape(b, t, H, K)
            vh = (kv_in @ wv + bv).reshape(b, t, H, K)
            kh = jnp.concatenate([kh, jnp.broadcast_to(bias_k, (b, 1, H, K))], axis=1)
            vh = jnp.concatenate([vh, jnp.broadcast_to(bias_v, (b, 1, H, K))], axis=1)
            scale = jnp.sqrt(jnp.asarray(K, q_in.dtype))
            logits = jnp.einsum('bqhk,bthk->bhqt', qh, kh) / scale
            weights = jax.nn.softmax(logits, axis=-1)
            ctx = jnp.einsum('bhqt,bthk->bqhk', weights, vh).reshape(b, q_len, H * K)
            return ctx @ wo + bo

        def _forward(x, xf_1, xf_2, ln1_scale, ln1_offset, wq1, bq1, wk1, bk1, wv1, bv1, wo1, bo1, bias_k1, bias_v1, ln2_scale, ln2_offset, wq2, bq2, wk2, bk2, wv2, bv2, wo2, bo2, bias_k2, bias_v2, ln_mlp_scale, ln_mlp_offset, w_fc1, b_fc1, w_fc2, b_fc2):
            res = x
            h = _layer_norm(x, ln1_scale, ln1_offset)
            x = res + _cross_attention(h, xf_1, wq1, bq1, wk1, bk1, wv1, bv1, wo1, bo1, bias_k1, bias_v1)
            res = x
            h = _layer_norm(x, ln2_scale, ln2_offset)
            x = res + _cross_attention(h, xf_2, wq2, bq2, wk2, bk2, wv2, bv2, wo2, bo2, bias_k2, bias_v2)
            h = _layer_norm(x, ln_mlp_scale, ln_mlp_offset)
            h = jax.nn.gelu(h @ w_fc1 + b_fc1, approximate=False) @ w_fc2 + b_fc2
            return x + h
        return _forward(x, xf_1, xf_2, ln1_scale, ln1_offset, wq1, bq1, wk1, bk1, wv1, bv1, wo1, bo1, bias_k1, bias_v1, ln2_scale, ln2_offset, wq2, bq2, wk2, bk2, wv2, bv2, wo2, bo2, bias_k2, bias_v2, ln_mlp_scale, ln_mlp_offset, w_fc1, b_fc1, w_fc2, b_fc2)
    x = _L0_xattn_ref(x, ctx_2048, ctx_2048, L0_xattn_ln1_scale, L0_xattn_ln1_offset, L0_xattn_wq1, L0_xattn_bq1, L0_xattn_wk1, L0_xattn_bk1, L0_xattn_wv1, L0_xattn_bv1, L0_xattn_wo1, L0_xattn_bo1, L0_xattn_bias_k1, L0_xattn_bias_v1, L0_xattn_ln2_scale, L0_xattn_ln2_offset, L0_xattn_wq2, L0_xattn_bq2, L0_xattn_wk2, L0_xattn_bk2, L0_xattn_wv2, L0_xattn_bv2, L0_xattn_wo2, L0_xattn_bo2, L0_xattn_bias_k2, L0_xattn_bias_v2, L0_xattn_ln_mlp_scale, L0_xattn_ln_mlp_offset, L0_xattn_w_fc1, L0_xattn_b_fc1, L0_xattn_w_fc2, L0_xattn_b_fc2)
    return x

_drawn_inputs = setup_inputs


def setup_inputs(seed=0):
    import zlib

    import numpy as np

    out = dict(_drawn_inputs(seed))
    spreads = {'L0_xattn_ln1_scale': (1.0, 0.6),
     'L0_xattn_ln1_offset': (0.0, 0.8),
     'L0_xattn_bq1': (0.0, 0.8),
     'L0_xattn_bk1': (0.0, 2.0),
     'L0_xattn_bv1': (0.0, 0.1),
     'L0_xattn_bo1': (0.0, 0.1),
     'L0_xattn_ln2_scale': (1.0, 0.6),
     'L0_xattn_ln2_offset': (0.0, 0.8),
     'L0_xattn_bq2': (0.0, 0.8),
     'L0_xattn_bk2': (0.0, 2.0),
     'L0_xattn_bv2': (0.0, 0.1),
     'L0_xattn_bo2': (0.0, 0.1),
     'L0_xattn_ln_mlp_scale': (1.0, 0.2),
     'L0_xattn_ln_mlp_offset': (0.0, 0.351),
     'L0_xattn_b_fc1': (0.0, 0.1),
     'L0_xattn_b_fc2': (0.0, 0.1)}
    factors = {'L0_xattn_wq1': 3.474,
     'L0_xattn_wk1': 3.381,
     'L0_xattn_bias_k1': 64.0,
     'L0_xattn_bias_v1': 43.938,
     'L0_xattn_wq2': 3.587,
     'L0_xattn_wk2': 3.504,
     'L0_xattn_bias_k2': 64.0,
     'L0_xattn_bias_v2': 64.0}
    for name, (base, spread) in spreads.items():
        noise = np.random.default_rng([zlib.crc32(name.encode()), seed]).standard_normal(out[name].shape)
        drawn = base * np.exp(spread * noise) if base else spread * noise
        out[name] = jnp.asarray(drawn.astype(out[name].dtype))
    for name, factor in factors.items():
        out[name] = (out[name] * factor).astype(out[name].dtype)
    return out
```

```python
import concourse.bass as bass
from concourse import mybir
from contextlib import ExitStack

F32 = mybir.dt.float32
F16 = mybir.dt.float16
U32 = mybir.dt.uint32
ALU = mybir.AluOpType
ACT = mybir.ActivationFunctionType
AX = mybir.AxisListType
RMAX = bass.bass_isa.ReduceOp.max

P = 128
B, Q, S, D, H, K, F = 4, 512, 64, 512, 16, 128, 2048
LAYERS = 2
C = D // P
TPB = Q // P
NT_ALL = B * TPB
HS = H * S
BS = B * S
J = HS // P
FC = F // P
BLK = 512
MB = B * C * HS // BLK
SPARE = 2
EPS = 1e-5
QK_SCALE = float(K) ** -0.5
TOP = 2.0 ** 14
LN_MAX = 23.0
EXP_MASK = 0x7F800000
V_BQ, V_BK, V_BV, V_BIASK, V_BIASV, V_LNS, V_LNO = 0, H, 2 * H, 3 * H, 4 * H, 5 * H, 5 * H + C
V_LAYER = 5 * H + 2 * C
V_MLP = LAYERS * V_LAYER
V_ALL = V_MLP + 2 * C + FC


def wait_past(eng, sem, count):
    if not isinstance(count, int) or count > 0:
        eng.wait_ge(sem, count)


def alone(eng, passed):
    eng.sem_inc(passed, 1)


def program(nc, x_d, ctx_d, wkq_d, wvo_d, vec_d, rows_d, w1_d, w2_d, y_d):
    with ExitStack() as ctx:
        def sb(name, shape, dt=F32):
            return ctx.enter_context(nc.sbuf_tensor(name, shape, dt))

        def sem(name):
            return ctx.enter_context(nc.semaphore(name))

        store = sb("store", [P, (2 * MB + SPARE) * BLK])
        x = sb("x", [P, NT_ALL, D])
        qk_bias = sb("qk_bias", [P, B * HS])
        ring_or_ls = sb("ring_or_ls", [P, 2, 2 * D])
        ctx_or_pt = sb("ctx_or_pt", [P, C * BS])
        kv = sb("kv", [P, 2, BS])
        hT = sb("hT", [P, 2, 2, C, P], F16)
        xh = sb("xh", [P, D])
        crow = sb("crow", [P, D])
        ident = sb("ident", [P, P])
        ones = sb("ones", [P, P])
        vec = sb("vec", [P, V_ALL])
        kvb = sb("kvb", [P, LAYERS, 2, H])
        bq_now = sb("bq_now", [P, 2])
        lnv = sb("lnv", [P, LAYERS + 1, 2 * C])
        neg_half = sb("neg_half", [P, 1])
        stats = sb("stats", [P, 6])
        mv = sb("mv", [P, 2])
        ve = sb("ve", [P, 1])
        rstd = sb("rstd", [P, 1])
        top = sb("top", [P, 2, H])
        etop = sb("etop", [P, 2, H])
        tot = sb("tot", [P, 2, H])
        mx = sb("mx", [P, 2, H])
        lm = sb("lm", [P, 8])
        gm = sb("gm", [P, 8])
        up = sb("up", [P, 16])
        dn = sb("dn", [P, 16])
        UP_LN, UP_M, UP_VW, UP_W1, UP_W2, UP_G = 0, 3, 4, 5, 6, 7
        DN_L, DN_VW, DN_F1, DN_F2 = 8, 9, 10, 11
        bound = sb("bound", [P, 4])

        ring = [ring_or_ls[:, s] for s in range(2)]
        ls = [ring_or_ls[:, s] for s in range(2)]
        cT = ctx_or_pt[:].rearrange("p (c s) -> p c s", c=C)
        pt = ctx_or_pt[:].bitcast(F16).rearrange("p (a n) -> p a n", a=2)
        halves = store[:].bitcast(F16)
        m_out = store[:, SPARE * BLK:(SPARE + MB) * BLK].rearrange("p (b c n) -> p c b n", b=B, c=C)
        m_cols = store[:, SPARE * BLK:(SPARE + MB) * BLK].rearrange("p (g n) -> p g n", g=B * C)
        vw_out = store[:, (SPARE + MB) * BLK:].rearrange("p (b j n) -> p b j n", b=B, j=J)
        g32 = qk_bias[:, 0:2 * Q].rearrange("p (s n) -> p s n", s=2)
        gh = qk_bias[:, 2 * Q:4 * Q].bitcast(F16).rearrange("p (s a n) -> p s a n", s=2, a=2)

        pairs = [ctx.enter_context(nc.psum_tensor(f"pair{s}", [P, 2 * BLK], F32)) for s in range(2)]
        singles = [ctx.enter_context(nc.psum_tensor(f"single{s}", [P, 2 * BLK], F32)) for s in range(1)]
        ptp = singles[0]
        acc = ctx.enter_context(nc.psum_tensor("acc", [P, BLK], F32))
        ntp = ctx.enter_context(nc.psum_tensor("ntp", [P, BLK], F32))

        s_vec = sem("s_vec")
        s_x = [sem(f"s_x{b}") for b in range(B)]
        s_ctx = sem("s_ctx")
        s_ring = [sem(f"s_ring{s}") for s in range(2)]
        s_row = sem("s_row")
        s_w1 = sem("s_w1")
        s_w2 = sem("s_w2")
        s_out = sem("s_out")
        s_ident0 = sem("s_ident0")
        s_const = sem("s_const")
        s_acc0 = sem("s_acc0")
        s_dve = sem("s_dve")
        s_dve_loop = sem("s_dve_loop")
        s_lm = sem("s_lm")
        s_gm = sem("s_gm")
        s_up = sem("s_up")
        s_kv_mm = sem("s_kv_mm")
        s_kv = sem("s_kv")
        s_qkb_mm = sem("s_qkb_mm")
        s_qkb = sem("s_qkb")
        s_prep_mm = sem("s_prep_mm")
        s_prep = sem("s_prep")
        s_mag = sem("s_mag")
        s_crow = sem("s_crow")
        s_crow_mm = sem("s_crow_mm")
        s_crow_ok = sem("s_crow_ok")
        s_hi = sem("s_hi")
        s_lo = sem("s_lo")
        s_bn = sem("s_bn")
        s_mv = sem("s_mv")
        s_ve = sem("s_ve")
        s_rstd = sem("s_rstd")
        s_xh = sem("s_xh")
        s_nt = sem("s_nt")
        s_h32 = sem("s_h32")
        s_hhi = sem("s_hhi")
        s_h = sem("s_h")
        s_L = sem("s_L")
        s_ls = sem("s_ls")
        s_top0 = sem("s_top0")
        s_top = sem("s_top")
        s_etop = sem("s_etop")
        s_sub = sem("s_sub")
        s_exp = sem("s_exp")
        s_sum = sem("s_sum")
        s_tot = sem("s_tot")
        s_tot2 = sem("s_tot2")
        s_rc = sem("s_rc")
        s_prob = sem("s_prob")
        s_tp = sem("s_tp")
        s_pt_hi = sem("s_pt_hi")
        s_pt = sem("s_pt")
        s_pv = sem("s_pv")
        s_xc = sem("s_xc")
        s_xr = sem("s_xr")
        s_fc1 = sem("s_fc1")
        s_gelu = sem("s_gelu")
        s_ghi = sem("s_ghi")
        s_g = sem("s_g")
        s_fc2 = sem("s_fc2")
        s_y = sem("s_y")

        s_passed = [sem(f"s_passed{e}") for e in range(3)]

        block = ctx.enter_context(nc.Block())

        def prep_use(l, phase, h):
            return 2 * H * l + H * phase + h

        def split_base(l, what):
            return 2 * MB * l + MB * what

        LOOP_T0, LOOP_STEPS = 2, NT_ALL - 4

        def mlp_rows_at(b, half):
            at = (2 * MB + 2 * J * b + J + C * half) * BLK
            return halves[:, bass.ds(at, C * Q)].rearrange("p (c t) -> p c t", c=C)

        def mlp_dst(b, half, q):
            return mlp_rows_at(b, half)[:, :, q * P:(q + 1) * P]

        @block.sync
        def _(sp):
            sp.dma_start(vec[:], vec_d).then_inc(s_vec, 16)
            sp.dma_start(ctx_or_pt[:], ctx_d).then_inc(s_ctx, 16)
            x_v = x_d.rearrange("(i p) d -> p i d", p=P)
            y_v = y_d.rearrange("(i p) d -> p i d", p=P)

            def load_weights(l, phase, h, slot, r):
                wait_past(sp, s_prep_mm, prep_use(l, phase, h) - 1)
                alone(sp, s_passed[2])
                src = (wkq_d, wvo_d)[phase][l, h]
                sp.dma_start(ring[slot], src).then_inc(s_ring[slot], 16)

            for l in range(LAYERS):
                if l:
                    sp.wait_ge(s_tp, 2 * (NT_ALL * l - 1))
                    load_weights(l, 0, 0, 0, 0)
                    sp.wait_ge(s_pv, NT_ALL * l)
                    sp.dma_start(ctx_or_pt[:], ctx_d).then_inc(s_ctx, 16)
                    load_weights(l, 0, 1, 1, 0)
                else:
                    load_weights(l, 0, 0, 0, 0)
                    load_weights(l, 0, 1, 1, 0)
                    for b in range(B):
                        sp.dma_start(x[:, b * TPB:(b + 1) * TPB, :],
                                     x_v[:, b * TPB:(b + 1) * TPB, :]).then_inc(s_x[b], 16)
                sp.wait_ge(s_acc0, l + 1)
                sp.dma_start(crow[0:1, :], rows_d[l:l + 1, :]).then_inc(s_row, 16)
                with sp.Fori(1, H // 2) as r:
                    for j in range(2):
                        load_weights(l, 0, 2 * r + j, j, r)
                load_weights(l, 1, 0, 0, 0)
                load_weights(l, 1, 1, 1, 0)
                with sp.Fori(1, H // 2) as r:
                    for j in range(2):
                        sp.wait_ge(s_crow, H * l + 2 * r + j - 1)
                        alone(sp, s_passed[2])
                        load_weights(l, 1, 2 * r + j, j, r)
            sp.wait_ge(s_L, NT_ALL * LAYERS - TPB)
            sp.dma_start(store[:, SPARE * BLK:(SPARE + FC) * BLK], w1_d).then_inc(s_w1, 16)
            sp.wait_ge(s_L, NT_ALL * LAYERS)
            sp.dma_start(store[:, (SPARE + FC) * BLK:(SPARE + 2 * FC) * BLK], w2_d).then_inc(s_w2, 16)
            sp.wait_ge(s_xc, NT_ALL * LAYERS)
            sp.dma_start(crow[:], rows_d[LAYERS:LAYERS + 1, :].to_broadcast([P, D])).then_inc(s_row, 16)
            with sp.Fori(0, NT_ALL) as i:
                sp.wait_ge(s_y, i + 1)
                alone(sp, s_passed[2])
                sp.dma_start(y_v[:, bass.ds(i, 1), :].squeeze(1), x[:, bass.ds(i, 1), :].squeeze(1)).then_inc(s_out, 16)
            sp.wait_ge(s_out, 16 * NT_ALL)

        @block.gpsimd
        def _(pool):
            g = nc.gpsimd
            g.memset(neg_half[:], -0.5)
            g.memset(ones[:], 1.0)
            g.memset(ident[:], 0.0).then_inc(s_ident0, 1)
            pool.wait_ge(s_ident0, 1)
            g.affine_select(out=ident[:], in_=ident[:], compare_op=ALU.not_equal, fill=1.0, base=0,
                            pattern=[[-1, P]], channel_multiplier=1).then_inc(s_const, 1)

            def all_max(n, count, cols=1):
                pool.wait_ge(s_lm, count)
                g.partition_all_reduce(gm[:, 0:cols], lm[:, 0:cols], P, RMAX).then_inc(s_gm, 1)

            def split_hi(base, k, col):
                wait_past(pool, s_lo, base + k - 1)
                hi, src = halves[:, bass.ds(k * 2 * BLK, BLK)], store[:, bass.ds((k + SPARE) * BLK, BLK)]
                if isinstance(k, int):
                    g.tensor_scalar(hi, src, up[:, col:col + 1], 1.0, ALU.mult, ALU.mult).then_inc(s_hi, 1)
                else:
                    alone(pool, s_passed[0])
                    g.tensor_tensor(hi, src, up[:, col:col + 1].to_broadcast([P, BLK]), ALU.mult).then_inc(s_hi, 1)

            def rstd_of(n):
                pool.wait_ge(s_mv, n + 1)
                alone(pool, s_passed[0])
                g.tensor_scalar(ve[:], mv[:, 1:2], EPS, 1.0, ALU.add, ALU.mult).then_inc(s_ve, 1)
                pool.wait_ge(s_ve, n + 1)
                g.tensor_tensor(rstd[:], ve[:], neg_half[:], ALU.pow).then_inc(s_rstd, 1)

            def split_h(n, hi, lo, moves=False):
                pool.wait_ge(s_h32, n + 1)
                alone(pool, s_passed[0])
                src = xh[:].rearrange("p (c q) -> p c q", c=C)
                if moves:
                    g.tensor_tensor(hi, src, ones[:].unsqueeze(1).to_broadcast([P, C, P]), ALU.mult).then_inc(s_hhi, 1)
                else:
                    g.tensor_scalar(hi, src, 1.0, 1.0, ALU.mult, ALU.mult).then_inc(s_hhi, 1)
                pool.wait_ge(s_hhi, n + 1)
                alone(pool, s_passed[0])
                g.tensor_tensor(lo, src, hi, ALU.subtract).then_inc(s_h, 1)

            def add_crow(n, tile, ready):
                pool.wait_ge(s_xh, n + 1)
                if ready > LAYERS:
                    pool.wait_ge(s_row, 16 * ready)
                else:
                    pool.wait_ge(s_crow_ok, ready)
                alone(pool, s_passed[0])
                g.tensor_tensor(x[:, bass.ds(tile, 1), :].squeeze(1), x[:, bass.ds(tile, 1), :].squeeze(1), crow[:], ALU.add).then_inc(s_xc, 1)

            for l in range(LAYERS):
                base = NT_ALL * l
                wait_past(pool, s_xc, NT_ALL * l)
                g.memset(crow[:], 0.0).then_inc(s_acc0, 1)
                if l == 0:
                    all_max(6, 1, cols=6)
                all_max(1, 2 + 2 * l)
                pool.wait_ge(s_up, 2 + 2 * l)
                for k in range(4):
                    split_hi(split_base(l, 0), k, UP_M)
                with pool.Fori(1, H // 2 - 1) as r:
                    for k in range(4):
                        split_hi(split_base(l, 0), 4 * r + k, UP_M)
                rstd_of(base)
                split_h(base, hT[:, 0, 0], hT[:, 0, 1])
                for k in range(MB - 4, MB):
                    split_hi(split_base(l, 0), k, UP_M)
                rstd_of(base + 1)
                all_max(1, 3 + 2 * l)
                pool.wait_ge(s_up, 3 + 2 * l)
                for k in range(MB, MB + J):
                    split_hi(split_base(l, 0), k, UP_VW)

                def pool_step(r, t, slot_t):
                    if LOOP_T0 <= t < LOOP_T0 + LOOP_STEPS:
                        for k in range(2):
                            split_hi(split_base(l, 0), MB + J + 8 * r + 2 * (t - LOOP_T0) + k, UP_VW)
                    if t + 2 < NT_ALL:
                        n = 4 * r + t + 2
                        if t + 2 > 1:
                            rstd_of(base + n)
                        wait_past(pool, s_L, base + n - 1)
                        split_h(base + n, hT[:, t % 2, 0], hT[:, t % 2, 1])
                    if t == -1:
                        add_crow(base, 0, l + 1)
                    if t + 2 < NT_ALL:
                        add_crow(base + 4 * r + t + 2, 4 * r + t + 2, l + 1)
                    if t + 1 < NT_ALL:
                        n = base + 4 * r + t + 1
                        pool.wait_ge(s_rc, n + 1)
                        v = ls[(t + 1) % 2].rearrange("p (h s) -> p h s", h=H)
                        g.tensor_tensor(v, v, tot[:, (t + 1) % 2, :].unsqueeze(2).to_broadcast([P, H, S]),
                                        ALU.mult).then_inc(s_prob, 1)

                for t in (-1, 0, 1):
                    pool_step(0, t, t)
                with pool.Fori(0, LOOP_STEPS // 4) as r:
                    for j in range(4):
                        pool_step(r, LOOP_T0 + j, j)
                for t in (14, 15, 16):
                    pool_step(0, t, t)

            base = NT_ALL * LAYERS

            def mlp_rows(b, q):
                n = base + TPB * b + q
                rstd_of(n)
                split_h(n, mlp_dst(b, 0, q), mlp_dst(b, 1, q), not isinstance(b, int))
                add_crow(n, TPB * b + q, LAYERS + 1)

            all_max(1, 2 + 2 * LAYERS, cols=2)
            pool.wait_ge(s_up, 2 + 2 * LAYERS)
            for q in range(TPB):
                mlp_rows(0, q)
            for k in range(FC):
                split_hi(split_base(LAYERS, 0), k, UP_W1)
            all_max(1, 3 + 2 * LAYERS)
            pool.wait_ge(s_up, 3 + 2 * LAYERS)
            for k in range(FC):
                split_hi(split_base(LAYERS, 0), FC + k, UP_W2)

            def pool_batch(b, more):
                for f in range(FC):
                    n = FC * b + f
                    if more and f % 4 == 1:
                        mlp_rows(b + 1, f // 4)
                    pool.wait_ge(s_gelu, n + 1)
                    if f >= 2 or not isinstance(b, int) or b > 0:
                        if isinstance(b, int) or f >= 2:
                            pool.wait_ge(s_fc2, n - 1)
                    alone(pool, s_passed[0])
                    g.tensor_scalar(gh[:, f % 2, 0], g32[:, f % 2], up[:, UP_G:UP_G + 1], 1.0,
                                    ALU.mult, ALU.mult).then_inc(s_ghi, 1)

            pool_batch(0, True)
            with pool.Fori(1, B - 1) as b:
                pool_batch(b, True)
            pool_batch(B - 1, False)

        @block.scalar
        def _(act):
            a = nc.scalar
            act.wait_ge(s_vec, 16)
            act.wait_ge(s_up, 1)

            def head_kv(l, phase, h, slot):
                u = prep_use(l, phase, h)
                act.wait_ge(s_kv_mm, u + 1)
                wait_past(act, s_prep_mm, u - 1)
                if phase == 0:
                    o = l * V_LAYER + V_BQ
                    a.activation(bq_now[:, slot:slot + 1], col(vec[:, o:o + H], h), ACT.Copy)
                a.activation(kv[:, slot], ptp[:, slot * BLK:slot * BLK + BS], ACT.Identity,
                             bias=col(kvb[:, l, phase], h)).then_inc(s_kv, 1)

            def col(v, h):
                return v[:, bass.ds(h, 1)]

            def head_m(l, h, slot):
                n = H * l + h
                act.wait_ge(s_qkb_mm, n + 1)
                a.activation(qk_bias[:].rearrange("p (b n) -> p b n", b=B)[:, :, bass.ds(h * S, S)],
                             acc[:, 0:BS].rearrange("p (b s) -> p b s", b=B), ACT.Copy,
                             scale=QK_SCALE).then_inc(s_qkb, 1)
                act.wait_ge(s_prep_mm, prep_use(l, 0, h) + 1)
                a.activation(m_out[:, :, :, bass.ds(h * S, S)],
                             pairs[slot][:].rearrange("p (c b s) -> p c b s", c=C, b=B),
                             ACT.Copy).then_inc(s_prep, 1)

            def head_vw(l, h, hh, slot):
                act.wait_ge(s_prep_mm, prep_use(l, 1, h) + 1)
                for par in range(2):
                    src = pairs[slot][S * par:S * (par + 1), :].rearrange("p (g n) -> p g n", g=2)
                    last = a.activation(vw_out[S * slot:S * (slot + 1), par::2, hh, :], src, ACT.Copy)
                last.then_inc(s_prep, 1)

            def affine(n, vector):
                act.wait_ge(s_nt, n + 1)
                for c in range(C):
                    last = a.activation(xh[:, c * P:(c + 1) * P], ntp[:, c * P:(c + 1) * P], ACT.Identity,
                                        scale=lnv[:, vector, c:c + 1], bias=lnv[:, vector, C + c:C + c + 1])
                last.then_inc(s_h32, 1)

            for l in range(LAYERS):
                base = NT_ALL * l
                head_kv(l, 0, 0, 0)
                for h in range(2):
                    head_kv(l, 0, h + 1, (h + 1) % 2)
                    head_m(l, h, h % 2)
                with act.Fori(1, H // 2 - 1) as r:
                    for j in range(2):
                        head_kv(l, 0, 2 * r + j + 1, (j + 1) % 2)
                        head_m(l, 2 * r + j, j)
                head_kv(l, 0, H - 1, 1)
                head_m(l, H - 2, 0)
                head_kv(l, 1, 0, 0)
                head_m(l, H - 1, 1)
                with act.Fori(0, H // 2 - 1) as r:
                    for j in range(2):
                        head_kv(l, 1, 2 * r + j + 1, (j + 1) % 2)
                        head_vw(l, 2 * r + j, r, j)
                affine(base, l)
                head_kv(l, 1, H - 1, 1)
                head_vw(l, H - 2, H // 2 - 1, 0)
                head_vw(l, H - 1, H // 2 - 1, 1)
                act.wait_ge(s_crow_mm, l + 1)
                a.activation(crow[:], acc[:], ACT.Copy).then_inc(s_crow_ok, 1)

                def act_step(r, t):
                    if t >= 1:
                        n = base + 4 * r + t - 1
                        for k in range(2):
                            act.wait_ge(s_tp, 2 * n + k + 1)
                            wait_past(act, s_pv, n)
                            a.activation(pt[:, 0, k * BLK:(k + 1) * BLK], ptp[:, k * BLK:(k + 1) * BLK],
                                         ACT.Copy).then_inc(s_pt_hi, 1)
                    if t + 2 < NT_ALL:
                        affine(base + 4 * r + t + 2, l)
                    if t + 1 < NT_ALL:
                        n = base + 4 * r + t + 1
                        slot = (t + 1) % 2
                        act.wait_ge(s_top, n + 1)
                        a.activation(etop[:, slot], top[:, slot], ACT.Exp, scale=-1.0).then_inc(s_etop, 1)
                        act.wait_ge(s_sub, n + 1)
                        a.activation(ls[slot], ls[slot], ACT.Exp).then_inc(s_exp, 1)

                for t in (-1, 0, 1):
                    act_step(0, t)
                with act.Fori(0, LOOP_STEPS // 4) as r:
                    for j in range(4):
                        act_step(r, LOOP_T0 + j)
                for t in (14, 15, 16):
                    act_step(0, t)

            base = NT_ALL * LAYERS
            for q in range(TPB):
                affine(base + q, LAYERS)

            def act_batch(b, more):
                for f in range(FC):
                    n = FC * b + f
                    if more and f % 4 == 1:
                        affine(base + TPB * (b + 1) + f // 4, LAYERS)
                    act.wait_ge(s_fc1, n + 1)
                    if isinstance(b, int):
                        wait_past(act, s_g, n - 1)
                    else:
                        act.wait_ge(s_g, n - 1)
                    o = V_MLP + 2 * C + f
                    a.activation(g32[:, f % 2], ptp[:, (f % 2) * BLK:(f % 2 + 1) * BLK], ACT.Gelu,
                                 scale=dn[:, DN_F1:DN_F1 + 1], bias=vec[:, o:o + 1]).then_inc(s_gelu, 1)

            act.wait_ge(s_up, 2 + 2 * LAYERS)
            act_batch(0, True)
            with act.Fori(1, B - 1) as b:
                act_batch(b, True)
            act_batch(B - 1, False)

        @block.vector
        def _(dve):
            v = nc.vector
            chained = [0]

            def link(instruction):
                chained[0] += 1
                instruction.then_inc(s_dve, 1)
                dve.wait_ge(s_dve, chained[0])

            def power(src, at, n=1):
                p_ap = dn[:, at:at + n]
                link(v.tensor_scalar(p_ap.bitcast(U32), src.bitcast(U32), EXP_MASK, None, ALU.bitwise_and))
                link(v.tensor_scalar(p_ap, p_ap, 2.0 ** -80, None, ALU.max))
                link(v.reciprocal(up[:, at:at + n], p_ap))
                link(v.tensor_scalar(up[:, at:at + n], up[:, at:at + n], TOP, None, ALU.mult))
                return v.tensor_scalar(p_ap, p_ap, 1.0 / TOP, None, ALU.mult)

            dve.wait_ge(s_vec, 16)
            for l in range(LAYERS):
                o = l * V_LAYER
                v.tensor_tensor(kvb[:, l], vec[:, o + V_BK:o + V_BK + 2 * H].rearrange("p (a h) -> p a h", a=2),
                                vec[:, o + V_BIASK:o + V_BIASK + 2 * H].rearrange("p (a h) -> p a h", a=2),
                                ALU.subtract)
            ln_at = [V_LNS, V_LAYER + V_LNS, V_MLP]
            for n, o in enumerate(ln_at):
                last = v.tensor_reduce(lm[:, 2 * n:2 * n + 2], vec[:, o:o + 2 * C].rearrange("p (a c) -> p a c", a=2),
                                       AX.X, ALU.max, apply_absolute_value=True)
            last.then_inc(s_lm, 1)
            dve.wait_ge(s_gm, 1)
            for n in range(LAYERS + 1):
                last = v.scalar_tensor_tensor(bound[:, n:n + 1], gm[:, 2 * n:2 * n + 1], LN_MAX,
                                              gm[:, 2 * n + 1:2 * n + 2], ALU.mult, ALU.add)
            link(last)
            link(power(bound[:, 0:3], UP_LN, 3))
            for n, o in enumerate(ln_at):
                last = v.tensor_scalar(lnv[:, n], vec[:, o:o + 2 * C], up[:, UP_LN + n:UP_LN + n + 1], None, ALU.mult)
            last.then_inc(s_up, 1)

            def split_lo(base, k, src_col):
                dve.wait_ge(s_hi, base + k + 1)
                v.scalar_tensor_tensor(halves[:, bass.ds(k * 2 * BLK + BLK, BLK)],
                                       store[:, bass.ds((k + SPARE) * BLK, BLK)],
                                       up[:, src_col:src_col + 1], halves[:, bass.ds(k * 2 * BLK, BLK)],
                                       ALU.mult, ALU.subtract).then_inc(s_lo, 1)

            def norm_rows(n, tile, loaded=None):
                if loaded is not None:
                    dve.wait_ge(loaded, 16)
                else:
                    dve.wait_ge(s_xr, n - NT_ALL + 1)
                v.bn_stats(stats[:], x[:, bass.ds(tile, 1), :].squeeze(1)).then_inc(s_bn, 1)
                dve.wait_ge(s_bn, n + 1)
                alone(dve, s_passed[1])
                v.bn_aggr(mv[:], stats[:]).then_inc(s_mv, 1)
                dve.wait_ge(s_rstd, n + 1)
                wait_past(dve, s_h, n)
                v.tensor_scalar(xh[:], x[:, bass.ds(tile, 1), :].squeeze(1), mv[:, 0:1], rstd[:, 0:1], ALU.subtract,
                                ALU.mult).then_inc(s_xh, 1)

            def head_mag(l, h):
                dve.wait_ge(s_prep, prep_use(l, 0, h) + 1)
                v.tensor_reduce(mx[:, 0, bass.ds(h, 1)], m_cols[:, :, bass.ds(h * S, S)], AX.XY, ALU.max,
                                apply_absolute_value=True).then_inc(s_mag, 1)

            for l in range(LAYERS):
                base = NT_ALL * l
                mags = (H + J) * l
                with dve.Fori(0, H) as h:
                    head_mag(l, h)
                dve.wait_ge(s_mag, mags + H)
                v.tensor_reduce(lm[:, 0:1], mx[:, 0, :], AX.X, ALU.max).then_inc(s_lm, 1)
                dve.wait_ge(s_gm, 2 + 2 * l)
                link(power(gm[:, 0:1], UP_M))
                link(v.tensor_scalar(dn[:, DN_L:DN_L + 1], dn[:, UP_M:UP_M + 1], dn[:, UP_LN + l:UP_LN + l + 1],
                                     QK_SCALE, ALU.mult, ALU.mult))
                v.tensor_scalar(dn[:, DN_L:DN_L + 1], dn[:, DN_L:DN_L + 1], 1.0, None,
                                ALU.mult).then_inc(s_up, 1)
                dve.wait_ge(s_row, 16 * (l + 1))

                def v_heads(r, e):
                    for j in range(2):
                        dve.wait_ge(s_ring[j], 16 * (H * l + H // 2 + r + 1))
                        wait_past(dve, s_crow, H * l + 2 * r + j)
                        o = l * V_LAYER + V_BIASV
                        v.scalar_tensor_tensor(crow[:], ring[j][:, D:2 * D], vec[:, bass.ds(2 * r + (o + j), 1)],
                                               crow[:], ALU.mult, ALU.add).then_inc(s_crow, 1)
                        for k in range(2):
                            split_lo(split_base(l, 0), 4 * r + 2 * j + k, UP_M)
                    dve.wait_ge(s_prep, prep_use(l, 1, 2 * r + 1) + 1)
                    v.tensor_reduce(mx[:, 1, bass.ds(r, 1)], vw_out[:, :, r, :], AX.XY, ALU.max,
                                    apply_absolute_value=True).then_inc(s_mag, 1)

                if l == 0:
                    v_heads(0, 0)
                    with dve.Fori(1, H // 2 - 1) as r:
                        v_heads(r, r)
                else:
                    with dve.Fori(0, H // 2 - 1) as r:
                        v_heads(r, r)
                norm_rows(base, 0, s_x[0] if l == 0 else None)
                v_heads(H // 2 - 1, 0)
                norm_rows(base + 1, 1, s_x[0] if l == 0 else None)
                dve.wait_ge(s_mag, mags + H + J)
                v.tensor_reduce(lm[:, 0:1], mx[:, 1, 0:J], AX.X, ALU.max).then_inc(s_lm, 1)
                dve.wait_ge(s_gm, 3 + 2 * l)
                link(power(gm[:, 0:1], UP_VW))
                v.tensor_scalar(dn[:, DN_VW:DN_VW + 1], dn[:, UP_VW:UP_VW + 1], 1.0 / TOP, None,
                                ALU.mult).then_inc(s_up, 1)
                for k in range(MB, MB + J):
                    split_lo(split_base(l, 0), k, UP_VW)
                if l == 0:
                    for b in range(1, B):
                        dve.wait_ge(s_x[b], 16)

                def dve_step(r, t):
                    if t >= 1:
                        n = base + 4 * r + t - 1
                        for k in range(2):
                            dve.wait_ge(s_pt_hi, 2 * n + k + 1)
                            v.tensor_tensor(pt[:, 1, k * BLK:(k + 1) * BLK], ptp[:, k * BLK:(k + 1) * BLK],
                                            pt[:, 0, k * BLK:(k + 1) * BLK], ALU.subtract).then_inc(s_pt, 1)
                    if LOOP_T0 <= t < LOOP_T0 + LOOP_STEPS:
                        for k in range(2):
                            split_lo(split_base(l, 0), MB + J + 8 * r + 2 * (t - LOOP_T0) + k, UP_VW)
                    if 2 <= t + 2 < NT_ALL:
                        i = 4 * r + t + 2
                        norm_rows(base + i, i, s_x[0] if l == 0 else None)
                    slot = (t + 1) % 2
                    tops = top[:, slot].unsqueeze(2).to_broadcast([P, H, S])
                    if t + 1 < NT_ALL:
                        n = base + 4 * r + t + 1
                        heads = ls[slot].rearrange("p (h s) -> p h s", h=H)
                        b = r + (t + 1) // 4
                        dve.wait_ge(s_L, n + 1)
                        wait_past(dve, s_tp, 2 * (n - 1))
                        dve.wait_ge(s_qkb, H * (l + 1))
                        v.scalar_tensor_tensor(ls[slot], pairs[slot][:], dn[:, DN_L:DN_L + 1],
                                               qk_bias[:, bass.ds(b * HS, HS)], ALU.mult, ALU.add).then_inc(s_ls, 1)
                        dve.wait_ge(s_ls, n + 1)
                        v.tensor_reduce(top[:, slot], heads, AX.X, ALU.max).then_inc(s_top0, 1)
                        dve.wait_ge(s_top0, n + 1)
                        v.tensor_scalar(top[:, slot], top[:, slot], 0.0, None, ALU.max).then_inc(s_top, 1)
                        dve.wait_ge(s_top, n + 1)
                        v.tensor_tensor(heads, heads, tops, ALU.subtract).then_inc(s_sub, 1)
                    if t >= 1:
                        m = base + 4 * r + t - 1
                        i = 4 * r + t - 1
                        dve.wait_ge(s_pv, m + 1)
                        dve.wait_ge(s_xc, m + 1)
                        v.scalar_tensor_tensor(x[:, bass.ds(i, 1), :].squeeze(1), acc[:], dn[:, DN_VW:DN_VW + 1], x[:, bass.ds(i, 1), :].squeeze(1),
                                               ALU.mult, ALU.add).then_inc(s_xr, 1)
                    if t + 1 < NT_ALL:
                        n = base + 4 * r + t + 1
                        dve.wait_ge(s_exp, n + 1)
                        v.tensor_reduce(tot[:, slot], ls[slot].rearrange("p (h s) -> p h s", h=H), AX.X,
                                        ALU.add).then_inc(s_sum, 1)
                        dve.wait_ge(s_sum, n + 1)
                        dve.wait_ge(s_etop, n + 1)
                        v.tensor_tensor(tot[:, slot], tot[:, slot], etop[:, slot], ALU.add).then_inc(s_tot, 1)
                        dve.wait_ge(s_tot, n + 1)
                        v.tensor_scalar(tot[:, slot], tot[:, slot], 1.0 / TOP, None, ALU.mult).then_inc(s_tot2, 1)
                        dve.wait_ge(s_tot2, n + 1)
                        v.reciprocal(tot[:, slot], tot[:, slot]).then_inc(s_rc, 1)

                for t in (-1, 0, 1):
                    dve_step(0, t)
                with dve.Fori(0, LOOP_STEPS // 4) as r:
                    for j in range(4):
                        dve_step(r, LOOP_T0 + j)
                for t in (14, 15, 16):
                    dve_step(0, t)

            base = NT_ALL * LAYERS
            dve.wait_ge(s_w1, 16)
            v.tensor_reduce(lm[:, 1:2], vec[:, V_MLP + 2 * C:V_ALL], AX.X, ALU.max, apply_absolute_value=True)
            v.tensor_reduce(lm[:, 0:1], store[:, SPARE * BLK:(SPARE + FC) * BLK], AX.X, ALU.max,
                            apply_absolute_value=True).then_inc(s_lm, 1)
            dve.wait_ge(s_gm, 2 + 2 * LAYERS)
            link(power(gm[:, 0:1], UP_W1))
            link(v.tensor_scalar(bound[:, 3:4], gm[:, 0:1], bound[:, 2:3], float(D), ALU.mult, ALU.mult))
            link(v.tensor_tensor(bound[:, 3:4], bound[:, 3:4], gm[:, 1:2], ALU.add))
            link(power(bound[:, 3:4], UP_G))
            v.tensor_tensor(dn[:, DN_F1:DN_F1 + 1], dn[:, UP_W1:UP_W1 + 1],
                            dn[:, UP_LN + LAYERS:UP_LN + LAYERS + 1], ALU.mult).then_inc(s_up, 1)
            for q in range(TPB):
                norm_rows(base + q, q)
            with dve.Fori(0, FC // 4) as r:
                for k in range(4):
                    split_lo(split_base(LAYERS, 0), 4 * r + k, UP_W1)
            dve.wait_ge(s_w2, 16)
            v.tensor_reduce(lm[:, 0:1], store[:, (SPARE + FC) * BLK:(SPARE + 2 * FC) * BLK], AX.X, ALU.max,
                            apply_absolute_value=True).then_inc(s_lm, 1)
            dve.wait_ge(s_gm, 3 + 2 * LAYERS)
            link(power(gm[:, 0:1], UP_W2))
            v.tensor_tensor(dn[:, DN_F2:DN_F2 + 1], dn[:, UP_W2:UP_W2 + 1], dn[:, UP_G:UP_G + 1],
                            ALU.mult).then_inc(s_up, 1)
            with dve.Fori(0, FC // 4) as r:
                for k in range(4):
                    split_lo(split_base(LAYERS, 0), FC + 4 * r + k, UP_W2)

            def dve_batch(b, more):
                for f in range(FC):
                    n = FC * b + f
                    if more and f % 4 == 1:
                        q = f // 4
                        norm_rows(base + TPB * (b + 1) + q, TPB * (b + 1) + q)
                    dve.wait_ge(s_ghi, n + 1)
                    v.scalar_tensor_tensor(gh[:, f % 2, 1], g32[:, f % 2], up[:, UP_G:UP_G + 1], gh[:, f % 2, 0],
                                           ALU.mult, ALU.subtract).then_inc(s_g, 1)
                for q in range(TPB):
                    i = TPB * b + q
                    dve.wait_ge(s_fc2, FC * (b + 1))
                    dve.wait_ge(s_xc, base + i + 1)
                    v.scalar_tensor_tensor(x[:, bass.ds(i, 1), :].squeeze(1), pairs[q // 2][:, (q % 2) * BLK:(q % 2 + 1) * BLK],
                                           dn[:, DN_F2:DN_F2 + 1], x[:, bass.ds(i, 1), :].squeeze(1), ALU.mult, ALU.add).then_inc(s_y, 1)

            dve_batch(0, True)
            with dve.Fori(1, B - 1) as b:
                dve_batch(b, True)
            dve_batch(B - 1, False)

        @block.tensor
        def _(pe):
            t_ = nc.tensor

            def head_kv(l, phase, h, slot, slot_uses):
                u = prep_use(l, phase, h)
                pe.wait_ge(s_ring[slot], 16 * slot_uses)
                wait_past(pe, s_kv, u - 1)
                for c in range(C):
                    last = t_.matmul(ptp[:, slot * BLK:slot * BLK + BS], ring[slot][:, c * P:(c + 1) * P],
                                     cT[:, c, :], start=(c == 0), stop=(c == C - 1))
                last.then_inc(s_kv_mm, 1)

            def head_m(l, h, slot):
                u = prep_use(l, 0, h)
                pe.wait_ge(s_kv, u + 1)
                wait_past(pe, s_qkb, H * l + h)
                if isinstance(h, int) and h == 0:
                    wait_past(pe, s_xr, NT_ALL * l)
                t_.matmul(acc[:, 0:BS], bq_now[:, slot:slot + 1].to_broadcast([P, P]), kv[:, slot],
                          start=True, stop=True).then_inc(s_qkb_mm, 1)
                wait_past(pe, s_prep, u - 1)
                for c in range(C):
                    last = t_.matmul(pairs[slot][:, c * BS:(c + 1) * BS], ring[slot][:, D + c * P:D + (c + 1) * P],
                                     kv[:, slot], start=True, stop=True)
                last.then_inc(s_prep_mm, 1)

            def head_vw(l, h, slot):
                u = prep_use(l, 1, h)
                pe.wait_ge(s_kv, u + 1)
                pe.wait_ge(s_prep, u - 1)
                for g in range(2):
                    last = t_.matmul(pairs[slot][:, g * BLK:(g + 1) * BLK], kv[:, slot, g * P:(g + 1) * P],
                                     ring[slot][:, D:2 * D], start=True, stop=True)
                last.then_inc(s_prep_mm, 1)

            def transposes(n):
                pe.wait_ge(s_xh, n + 1)
                wait_past(pe, s_h32, n)
                for c in range(C):
                    last = t_.transpose(ntp[:, c * P:(c + 1) * P], xh[:, c * P:(c + 1) * P], ident[:])
                last.then_inc(s_nt, 1)

            pe.wait_ge(s_const, 1)
            for l in range(LAYERS):
                base = NT_ALL * l
                uses = H * l
                pe.wait_ge(s_ctx, 16 * (l + 1))
                head_kv(l, 0, 0, 0, uses + 1)
                for h in range(2):
                    head_kv(l, 0, h + 1, (h + 1) % 2, uses + (h + 1) // 2 + 1)
                    head_m(l, h, h % 2)
                with pe.Fori(1, H // 2 - 1) as r:
                    for j in range(2):
                        head_kv(l, 0, 2 * r + j + 1, (j + 1) % 2, uses + r + (j + 1) // 2 + 1)
                        head_m(l, 2 * r + j, j)
                head_kv(l, 0, H - 1, 1, uses + H // 2)
                head_m(l, H - 2, 0)
                head_kv(l, 1, 0, 0, uses + H // 2 + 1)
                head_m(l, H - 1, 1)
                with pe.Fori(0, H // 2 - 1) as r:
                    for j in range(2):
                        head_kv(l, 1, 2 * r + j + 1, (j + 1) % 2, uses + H // 2 + r + (j + 1) // 2 + 1)
                        head_vw(l, 2 * r + j, j)
                transposes(base)
                head_kv(l, 1, H - 1, 1, uses + H)
                head_vw(l, H - 2, 0)
                head_vw(l, H - 1, 1)
                pe.wait_ge(s_crow, H * (l + 1))
                pe.wait_ge(s_qkb, H * (l + 1))
                t_.matmul(acc[:], ones[:], crow[:], start=True, stop=True).then_inc(s_crow_mm, 1)
                pe.wait_ge(s_prep, prep_use(l + 1, 0, 0))

                def pe_step(r, t):
                    if t >= 1:
                        n = base + 4 * r + t - 1
                        pe.wait_ge(s_prob, n + 1)
                        wait_past(pe, s_pt, 2 * n)
                        for j in range(J):
                            tr = t_.transpose(ptp[:, j * P:(j + 1) * P], ls[(t - 1) % 2][:, j * P:(j + 1) * P], ident[:])
                            if j % 4 == 3:
                                tr.then_inc(s_tp, 1)
                    if t + 1 < NT_ALL:
                        n = base + 4 * r + t + 1
                        slot = (t + 1) % 2
                        b = r + (t + 1) // 4
                        pe.wait_ge(s_h, n + 1)
                        pe.wait_ge(s_lo, split_base(l, 0) + 2 * C * (b + 1))
                        wait_past(pe, s_ls, n - 1)
                        for c in range(C):
                            for half, mhalf in ((0, 0), (0, 1), (1, 0)):
                                for g in range(2):
                                    at = (b * 2 * C + 2 * c + g) * 2 * BLK + mhalf * BLK
                                    last = t_.matmul(pairs[slot][:, g * BLK:(g + 1) * BLK], hT[:, slot, half, c, :],
                                                     halves[:, bass.ds(at, BLK)], start=(c == 0 and half + mhalf == 0),
                                                     stop=(c == C - 1 and half == 1))
                        last.then_inc(s_L, 1)
                    if t + 2 < NT_ALL:
                        transposes(base + 4 * r + t + 2)
                    if t >= 1:
                        n = base + 4 * r + t - 1
                        b = r + (t - 1) // 4
                        pe.wait_ge(s_pt, 2 * n + 2)
                        pe.wait_ge(s_lo, split_base(l, 1) + J * (b + 1))
                        pe.wait_ge(s_crow_ok, l + 1)
                        wait_past(pe, s_xr, n)
                        for j in range(J):
                            for half, vhalf in ((0, 0), (0, 1), (1, 0)):
                                at = (MB + b * J + j) * 2 * BLK + vhalf * BLK
                                last = t_.matmul(acc[:], pt[:, half, j * P:(j + 1) * P], halves[:, bass.ds(at, BLK)],
                                                 start=(j == 0 and half + vhalf == 0), stop=(j == J - 1 and half == 1))
                        last.then_inc(s_pv, 1)

                for t in (-1, 0, 1):
                    pe_step(0, t)
                with pe.Fori(0, LOOP_STEPS // 4) as r:
                    for j in range(4):
                        pe_step(r, LOOP_T0 + j)
                for t in (14, 15, 16):
                    pe_step(0, t)

            base = NT_ALL * LAYERS
            for q in range(TPB):
                transposes(base + q)

            def fc1(b, f):
                n = FC * b + f
                if isinstance(b, int):
                    wait_past(pe, s_gelu, n - 1)
                else:
                    pe.wait_ge(s_gelu, n - 1)
                pe.wait_ge(s_lo, split_base(LAYERS, 0) + f + 1)
                pe.wait_ge(s_h, base + TPB * (b + 1))
                for c in range(C):
                    for whalf, half in ((0, 0), (0, 1), (1, 0)):
                        at = (f * 2 + whalf) * BLK + c * P
                        src = mlp_rows_at(b, half)[:, c, :]
                        last = t_.matmul(ptp[:, (f % 2) * BLK:(f % 2 + 1) * BLK], halves[:, at:at + P], src,
                                         start=(c == 0 and whalf + half == 0), stop=(c == C - 1 and whalf == 1))
                last.then_inc(s_fc1, 1)

            def fc2(b, f):
                n = FC * b + f
                pe.wait_ge(s_g, n + 1)
                pe.wait_ge(s_lo, split_base(LAYERS, 0) + FC + f + 1)
                if f == 0:
                    wait_past(pe, s_y, TPB * b)
                for q in range(TPB):
                    for half, whalf in ((0, 0), (0, 1), (1, 0)):
                        at = ((FC + f) * 2 + whalf) * BLK
                        last = t_.matmul(pairs[q // 2][:, (q % 2) * BLK:(q % 2 + 1) * BLK],
                                         gh[:, f % 2, half, q * P:(q + 1) * P], halves[:, bass.ds(at, BLK)],
                                         start=(f == 0 and half + whalf == 0), stop=(f == FC - 1 and half == 1))
                last.then_inc(s_fc2, 1)

            def pe_batch(b, more):
                fc1(b, 0)
                for f in range(FC):
                    if f + 1 < FC:
                        fc1(b, f + 1)
                    if more and f % 4 == 1:
                        transposes(base + TPB * (b + 1) + f // 4)
                    fc2(b, f)

            pe_batch(0, True)
            with pe.Fori(1, B - 1) as b:
                pe_batch(b, True)
            pe_batch(B - 1, False)


def kernel(**inputs):
    import numpy as np
    import concourse.bacc as bacc
    from concourse.bass_utils import run_bass_kernel_spmd

    w = {k.replace("L0_xattn_", ""): np.asarray(v) for k, v in inputs.items()}

    def by_chunk(v):
        return v.reshape(-1, P).T

    def heads_in(m):
        return m.reshape(C, P, H, K).transpose(2, 1, 0, 3).reshape(H, P, C * K)

    wkq = np.stack([np.concatenate([heads_in(w[f"wk{i}"]), w[f"wq{i}"].T.reshape(H, K, D)], axis=2) for i in (1, 2)])
    wvo = np.stack([np.concatenate([heads_in(w[f"wv{i}"]), w[f"wo{i}"].reshape(H, K, D)], axis=2) for i in (1, 2)])
    cols = []
    for i in (1, 2):
        for name in (f"bq{i}", f"bk{i}", f"bv{i}", f"bias_k{i}", f"bias_v{i}", f"ln{i}_scale", f"ln{i}_offset"):
            cols.append(by_chunk(w[name].reshape(-1)))
    for name in ("ln_mlp_scale", "ln_mlp_offset", "b_fc1"):
        cols.append(by_chunk(w[name]))
    arrays = {
        "x": w["x"].reshape(B * Q, D),
        "ctxT": w["ctx_2048"].reshape(BS, C, P).transpose(2, 1, 0).reshape(P, C * BS),
        "wkq": wkq,
        "wvo": wvo,
        "vectors": np.concatenate(cols, axis=1),
        "rows": np.stack([w["bo1"], w["bo2"], w["b_fc2"]]),
        "w1": w["w_fc1"].reshape(C, P, FC, P).transpose(1, 2, 0, 3).reshape(P, FC * D),
        "w2": w["w_fc2"].reshape(FC, P, D).transpose(1, 0, 2).reshape(P, FC * D),
    }
    arrays = {k: np.ascontiguousarray(v) for k, v in arrays.items()}
    nc = bacc.Bacc("TRN2", target_bir_lowering=False, num_devices=1)
    args = [nc.dram_tensor(k + "_dram", v.shape, F32, kind="ExternalInput").ap() for k, v in arrays.items()]
    args.append(nc.dram_tensor("y_dram", (B * Q, D), F32, kind="ExternalOutput").ap())
    program(nc, *args)
    r = run_bass_kernel_spmd(nc, [{k + "_dram": v for k, v in arrays.items()}], core_ids=[0])
    return np.asarray(r.results[0]["y_dram"]).reshape(B, Q, D)
```

```python
import concourse.bass as bass
from concourse import mybir
from contextlib import ExitStack

F32 = mybir.dt.float32
F16 = mybir.dt.float16
U32 = mybir.dt.uint32
ALU = mybir.AluOpType
ACT = mybir.ActivationFunctionType
AX = mybir.AxisListType
RMAX = bass.bass_isa.ReduceOp.max

P = 128
B, Q, S, D, H, K, F = 4, 512, 64, 512, 16, 128, 2048
LAYERS = 2
C = D // P
TPB = Q // P
NT_ALL = B * TPB
HS = H * S
BS = B * S
J = HS // P
FC = F // P
BLK = 512
MB = B * C * HS // BLK
SPARE = 2
WPARTS = 4
WB = FC // WPARTS
W2_AT = MB + 6
EPS = 1e-5
QK_SCALE = float(K) ** -0.5
TOP = 2.0 ** 14
LN_MAX = 23.0
EXP_MASK = 0x7F800000
MLP_AHEAD = 4
V_BQ, V_BK, V_BV, V_BIASK, V_BIASV, V_LNS, V_LNO = 0, H, 2 * H, 3 * H, 4 * H, 5 * H, 5 * H + C
V_LAYER = 5 * H + 2 * C
V_MLP = LAYERS * V_LAYER
V_ALL = V_MLP + 2 * C + FC


def wait_past(eng, sem, count):
    if not isinstance(count, int) or count > 0:
        eng.wait_ge(sem, count)


def alone(eng, passed):
    eng.sem_inc(passed, 1)


def program(nc, x_d, ctx_d, w_d, vec_d, rows_d, w12_d, y_d):
    with ExitStack() as ctx:
        def sb(name, shape, dt=F32):
            return ctx.enter_context(nc.sbuf_tensor(name, shape, dt))

        def sem(name):
            return ctx.enter_context(nc.semaphore(name))

        store = sb("store", [P, (2 * MB + SPARE) * BLK])
        x = sb("x", [P, NT_ALL, D])
        qk_bias = sb("qk_bias", [P, B * HS])
        ring_or_ls = sb("ring_or_ls", [P, 2, 2 * D])
        ctx_or_pt = sb("ctx_or_pt", [P, C * BS])
        kv = sb("kv", [P, 2, BS])
        hT = sb("hT", [P, 2, 2, C, P], F16)
        xh = sb("xh", [P, D])
        crow = sb("crow", [P, D])
        ident = sb("ident", [P, P])
        ones = sb("ones", [P, P])
        vec = sb("vec", [P, V_ALL])
        kvb = sb("kvb", [P, LAYERS, 2, H])
        bq_now = sb("bq_now", [P, 2])
        lnv = sb("lnv", [P, LAYERS + 1, 2 * C])
        neg_half = sb("neg_half", [P, 1])
        stats = sb("stats", [P, 6])
        mv = sb("mv", [P, 2])
        ve = sb("ve", [P, 1])
        rstd = sb("rstd", [P, 1])
        top = sb("top", [P, 2, H])
        etop = sb("etop", [P, 2, H])
        tot = sb("tot", [P, 2, H])
        mx = sb("mx", [P, 2, H])
        mw = sb("mw", [P, 2 * WPARTS])
        lm = sb("lm", [P, 8])
        gm = sb("gm", [P, 8])
        up = sb("up", [P, 16])
        dn = sb("dn", [P, 16])
        UP_LN, UP_M, UP_VW, UP_W1, UP_W2, UP_G = 0, 3, 4, 5, 6, 7
        DN_L, DN_VW, DN_F1, DN_F2 = 8, 9, 10, 11
        bound = sb("bound", [P, 4])

        ring = [ring_or_ls[:, s] for s in range(2)]
        ls = [ring_or_ls[:, s] for s in range(2)]
        cT = ctx_or_pt[:].rearrange("p (c s) -> p c s", c=C)
        pt = ctx_or_pt[:].bitcast(F16).rearrange("p (a n) -> p a n", a=2)
        halves = store[:].bitcast(F16)
        m_out = store[:, SPARE * BLK:(SPARE + MB) * BLK].rearrange("p (b c n) -> p c b n", b=B, c=C)
        m_cols = store[:, SPARE * BLK:(SPARE + MB) * BLK].rearrange("p (g n) -> p g n", g=B * C)
        vw_out = store[:, (SPARE + MB) * BLK:].rearrange("p (b j n) -> p b j n", b=B, j=J)
        g32 = qk_bias[:, 0:2 * Q].rearrange("p (s n) -> p s n", s=2)
        gh = qk_bias[:, 2 * Q:4 * Q].bitcast(F16).rearrange("p (s a n) -> p s a n", s=2, a=2)

        pairs = [ctx.enter_context(nc.psum_tensor(f"pair{s}", [P, 2 * BLK], F32)) for s in range(2)]
        singles = [ctx.enter_context(nc.psum_tensor(f"single{s}", [P, 2 * BLK], F32)) for s in range(1)]
        ptp = singles[0]
        acc = ctx.enter_context(nc.psum_tensor("acc", [P, BLK], F32))
        ntp = ctx.enter_context(nc.psum_tensor("ntp", [P, BLK], F32))

        s_vec = sem("s_vec")
        s_x = [sem(f"s_x{b}") for b in range(B)]
        s_ctx = sem("s_ctx")
        s_ring_a = [sem(f"s_ring_a{s}") for s in range(2)]
        s_ring_b = [sem(f"s_ring_b{s}") for s in range(2)]
        s_row = sem("s_row")
        s_wm = sem("s_wm")
        s_wm_mag = sem("s_wm_mag")
        s_w1 = [sem(f"s_w1_{n}") for n in range(WPARTS)]
        s_w2 = [sem(f"s_w2_{n}") for n in range(WPARTS)]
        s_out = sem("s_out")
        s_ident0 = sem("s_ident0")
        s_const = sem("s_const")
        s_acc0 = sem("s_acc0")
        s_dve = sem("s_dve")
        s_dve_loop = sem("s_dve_loop")
        s_lm = sem("s_lm")
        s_gm = sem("s_gm")
        s_up = sem("s_up")
        s_kv_mm = sem("s_kv_mm")
        s_kv = sem("s_kv")
        s_qkb_mm = sem("s_qkb_mm")
        s_qkb = sem("s_qkb")
        s_prep_mm = sem("s_prep_mm")
        s_prep = sem("s_prep")
        s_mag = sem("s_mag")
        s_crow = sem("s_crow")
        s_crow_mm = sem("s_crow_mm")
        s_crow_ok = sem("s_crow_ok")
        s_hi = sem("s_hi")
        s_lo = sem("s_lo")
        s_bn = sem("s_bn")
        s_mv = sem("s_mv")
        s_ve = sem("s_ve")
        s_rstd = sem("s_rstd")
        s_xh = sem("s_xh")
        s_nt = sem("s_nt")
        s_h32 = sem("s_h32")
        s_hhi = sem("s_hhi")
        s_h = sem("s_h")
        s_L = sem("s_L")
        s_ls = sem("s_ls")
        s_top0 = sem("s_top0")
        s_top = sem("s_top")
        s_etop = sem("s_etop")
        s_sub = sem("s_sub")
        s_exp = sem("s_exp")
        s_sum = sem("s_sum")
        s_tot = sem("s_tot")
        s_tot2 = sem("s_tot2")
        s_rc = sem("s_rc")
        s_prob = sem("s_prob")
        s_tp = sem("s_tp")
        s_pt_hi = sem("s_pt_hi")
        s_pt = sem("s_pt")
        s_pv = sem("s_pv")
        s_xc = sem("s_xc")
        s_xr = sem("s_xr")
        s_fc1 = sem("s_fc1")
        s_gelu = sem("s_gelu")
        s_ghi = sem("s_ghi")
        s_g = sem("s_g")
        s_fc2 = sem("s_fc2")
        s_y = sem("s_y")

        s_passed = [sem(f"s_passed{e}") for e in range(3)]

        block = ctx.enter_context(nc.Block())

        def prep_use(l, phase, h):
            return 2 * H * l + H * phase + h

        def split_base(l, what):
            return 2 * MB * l + MB * what

        LOOP_T0, LOOP_STEPS = 2, NT_ALL - 4

        def mlp_rows_at(b, half):
            slot = MB if isinstance(b, int) and b == 0 else FC + C * b
            at = (2 * slot + C * half) * BLK
            return halves[:, bass.ds(at, C * Q)].rearrange("p (c t) -> p c t", c=C)

        def mlp_dst(b, half, q):
            return mlp_rows_at(b, half)[:, :, q * P:(q + 1) * P]

        def mlp_block(k):
            if k < FC:
                return s_w1[k // WB], k, UP_W1
            return s_w2[(k - FC) // WB], W2_AT + k - FC, UP_W2

        def early_blocks(l, t):
            parts = {14: range(0, 6), 15: range(6, 12), 16: range(12, FC + MLP_AHEAD)}
            return parts.get(t, ()) if l == LAYERS - 1 else ()

        def late_blocks(f):
            return range(FC + MLP_AHEAD + f, min(FC + MLP_AHEAD + f + 1, 2 * FC))

        def early_rows(l, t):
            return {14: (0, 1), 15: (2,), 16: (3,)}.get(t, ()) if l == LAYERS - 1 else ()

        @block.sync
        def _(sp):
            sp.dma_start(vec[:], vec_d).then_inc(s_vec, 16)
            sp.dma_start(ctx_or_pt[:], ctx_d).then_inc(s_ctx, 16)
            x_v = x_d.rearrange("(i p) d -> p i d", p=P)
            y_v = y_d.rearrange("(i p) d -> p i d", p=P)

            def load_a(l, u, slot):
                wait_past(sp, s_kv_mm, 2 * H * l + u - 1)
                alone(sp, s_passed[2])
                sp.dma_start(ring[slot][:, 0:D], w_d[l, u][:, 0:D]).then_inc(s_ring_a[slot], 16)

            def load_b(l, u, slot, crow_too):
                if crow_too:
                    sp.wait_ge(s_crow, H * l + u - H - 1)
                    alone(sp, s_passed[2])
                wait_past(sp, s_prep_mm, 2 * H * l + u - 1)
                alone(sp, s_passed[2])
                sp.dma_start(ring[slot][:, D:2 * D], w_d[l, u][:, D:2 * D]).then_inc(s_ring_b[slot], 16)

            for l in range(LAYERS):
                if l:
                    sp.wait_ge(s_tp, 2 * (NT_ALL * l - 1))
                    load_a(l, 0, 0)
                    sp.wait_ge(s_tp, 2 * NT_ALL * l)
                    load_a(l, 1, 1)
                    sp.wait_ge(s_pv, NT_ALL * l)
                    sp.dma_start(ctx_or_pt[:], ctx_d).then_inc(s_ctx, 16)
                else:
                    load_a(l, 0, 0)
                    load_a(l, 1, 1)
                load_b(l, 0, 0, False)
                load_a(l, 2, 0)
                load_b(l, 1, 1, False)
                if l == 0:
                    for b in range(B):
                        sp.dma_start(x[:, b * TPB:(b + 1) * TPB, :],
                                     x_v[:, b * TPB:(b + 1) * TPB, :]).then_inc(s_x[b], 16)
                sp.wait_ge(s_acc0, l + 1)
                sp.dma_start(crow[0:1, :], rows_d[l:l + 1, :]).then_inc(s_row, 16)
                load_a(l, 3, 1)
                with sp.Fori(1, H // 2) as r:
                    for j in range(2):
                        load_b(l, 2 * r + j, j, False)
                        load_a(l, 2 * r + j + 2, j)
                for u in (H, H + 1):
                    load_b(l, u, u % 2, False)
                    load_a(l, u + 2, u % 2)
                with sp.Fori(H // 2 + 1, H - 1) as r:
                    for j in range(2):
                        load_b(l, 2 * r + j, j, True)
                        load_a(l, 2 * r + j + 2, j)
                for u in (2 * H - 2, 2 * H - 1):
                    load_b(l, u, u % 2, True)
            sp.wait_ge(s_L, NT_ALL * LAYERS - TPB)
            for n in range(WPARTS):
                at = (SPARE + n * WB) * BLK
                sp.dma_start(store[:, at:at + WB * BLK], w12_d[:, n * WB * BLK:(n + 1) * WB * BLK]).then_inc(s_w1[n], 16)
            sp.wait_ge(s_pv, NT_ALL * LAYERS - TPB)
            for n in range(WPARTS):
                at = (W2_AT + SPARE + n * WB) * BLK
                sp.dma_start(store[:, at:at + WB * BLK], w12_d[:, (FC + n * WB) * BLK:(FC + (n + 1) * WB) * BLK]).then_inc(s_w2[n], 16)
            sp.wait_ge(s_xc, NT_ALL * LAYERS)
            sp.dma_start(crow[:], rows_d[LAYERS:LAYERS + 1, :].to_broadcast([P, D])).then_inc(s_row, 16)
            with sp.Fori(0, NT_ALL) as i:
                sp.wait_ge(s_y, i + 1)
                alone(sp, s_passed[2])
                sp.dma_start(y_v[:, bass.ds(i, 1), :].squeeze(1), x[:, bass.ds(i, 1), :].squeeze(1)).then_inc(s_out, 16)
            sp.wait_ge(s_out, 16 * NT_ALL)

        @block.gpsimd
        def _(pool):
            g = nc.gpsimd
            g.memset(neg_half[:], -0.5)
            g.memset(ones[:], 1.0)
            g.memset(ident[:], 0.0).then_inc(s_ident0, 1)
            pool.wait_ge(s_ident0, 1)
            g.affine_select(out=ident[:], in_=ident[:], compare_op=ALU.not_equal, fill=1.0, base=0,
                            pattern=[[-1, P]], channel_multiplier=1).then_inc(s_const, 1)

            def all_max(n, count, cols=1):
                pool.wait_ge(s_lm, count)
                g.partition_all_reduce(gm[:, 0:cols], lm[:, 0:cols], P, RMAX).then_inc(s_gm, 1)

            def split_hi(count, slot, col):
                wait_past(pool, s_lo, count - 1)
                hi, src = halves[:, bass.ds(slot * 2 * BLK, BLK)], store[:, bass.ds((slot + SPARE) * BLK, BLK)]
                if isinstance(slot, int):
                    g.tensor_scalar(hi, src, up[:, col:col + 1], 1.0, ALU.mult, ALU.mult).then_inc(s_hi, 1)
                else:
                    alone(pool, s_passed[0])
                    g.tensor_tensor(hi, src, up[:, col:col + 1].to_broadcast([P, BLK]), ALU.mult).then_inc(s_hi, 1)

            def rstd_of(n):
                pool.wait_ge(s_mv, n + 1)
                alone(pool, s_passed[0])
                g.tensor_scalar(ve[:], mv[:, 1:2], EPS, 1.0, ALU.add, ALU.mult).then_inc(s_ve, 1)
                pool.wait_ge(s_ve, n + 1)
                g.tensor_tensor(rstd[:], ve[:], neg_half[:], ALU.pow).then_inc(s_rstd, 1)

            def split_h(n, hi, lo, moves=False):
                pool.wait_ge(s_h32, n + 1)
                alone(pool, s_passed[0])
                src = xh[:].rearrange("p (c q) -> p c q", c=C)
                if moves:
                    g.tensor_tensor(hi, src, ones[:].unsqueeze(1).to_broadcast([P, C, P]), ALU.mult).then_inc(s_hhi, 1)
                else:
                    g.tensor_scalar(hi, src, 1.0, 1.0, ALU.mult, ALU.mult).then_inc(s_hhi, 1)
                pool.wait_ge(s_hhi, n + 1)
                alone(pool, s_passed[0])
                g.tensor_tensor(lo, src, hi, ALU.subtract).then_inc(s_h, 1)

            def add_crow(n, tile, ready):
                pool.wait_ge(s_xh, n + 1)
                if ready > LAYERS:
                    pool.wait_ge(s_row, 16 * ready)
                else:
                    pool.wait_ge(s_crow_ok, ready)
                alone(pool, s_passed[0])
                g.tensor_tensor(x[:, bass.ds(tile, 1), :].squeeze(1), x[:, bass.ds(tile, 1), :].squeeze(1), crow[:], ALU.add).then_inc(s_xc, 1)

            def mlp_rows(b, q, part=None):
                n = NT_ALL * LAYERS + TPB * b + q
                if part in (None, 0):
                    rstd_of(n)
                if part in (None, 2):
                    split_h(n, mlp_dst(b, 0, q), mlp_dst(b, 1, q), not isinstance(b, int))
                if part in (None, 3):
                    add_crow(n, TPB * b + q, LAYERS + 1)

            def mlp_split(k):
                landed, slot, col = mlp_block(k)
                pool.wait_ge(landed, 16)
                split_hi(split_base(LAYERS, 0) + k, slot, col)

            for l in range(LAYERS):
                base = NT_ALL * l
                wait_past(pool, s_xc, NT_ALL * l)
                g.memset(crow[:], 0.0).then_inc(s_acc0, 1)
                if l == 0:
                    all_max(6, 1, cols=6)
                all_max(1, 2 + 2 * l, cols=1 if l else 4)
                pool.wait_ge(s_up, 2 + 2 * l)
                for k in range(4):
                    split_hi(split_base(l, 0) + k, k, UP_M)
                with pool.Fori(1, H // 2 - 1) as r:
                    for k in range(4):
                        split_hi(split_base(l, 0) + 4 * r + k, 4 * r + k, UP_M)
                rstd_of(base)
                split_h(base, hT[:, 0, 0], hT[:, 0, 1])
                for k in range(MB - 4, MB):
                    split_hi(split_base(l, 0) + k, k, UP_M)
                rstd_of(base + 1)
                all_max(1, 3 + 2 * l)
                pool.wait_ge(s_up, 3 + 2 * l)
                for k in range(MB, MB + J):
                    split_hi(split_base(l, 0) + k, k, UP_VW)

                def pool_step(r, t):
                    if LOOP_T0 <= t < LOOP_T0 + LOOP_STEPS:
                        for k in range(2):
                            split_hi(split_base(l, 0) + MB + J + 8 * r + 2 * (t - LOOP_T0) + k, MB + J + 8 * r + 2 * (t - LOOP_T0) + k, UP_VW)
                    if t + 2 < NT_ALL:
                        n = 4 * r + t + 2
                        if t + 2 > 1:
                            rstd_of(base + n)
                        wait_past(pool, s_L, base + n - 1)
                        split_h(base + n, hT[:, t % 2, 0], hT[:, t % 2, 1])
                    if t == -1:
                        add_crow(base, 0, l + 1)
                    if t + 2 < NT_ALL:
                        add_crow(base + 4 * r + t + 2, 4 * r + t + 2, l + 1)
                    for q in early_rows(l, t)[:1]:
                        mlp_rows(0, q)
                    if t + 1 < NT_ALL:
                        n = base + 4 * r + t + 1
                        pool.wait_ge(s_rc, n + 1)
                        v = ls[(t + 1) % 2].rearrange("p (h s) -> p h s", h=H)
                        g.tensor_tensor(v, v, tot[:, (t + 1) % 2, :].unsqueeze(2).to_broadcast([P, H, S]),
                                        ALU.mult).then_inc(s_prob, 1)
                    for k in early_blocks(l, t):
                        mlp_split(k)
                    for q in early_rows(l, t)[1:]:
                        mlp_rows(0, q)

                for t in (-1, 0, 1):
                    pool_step(0, t)
                with pool.Fori(0, LOOP_STEPS // 4) as r:
                    for j in range(4):
                        pool_step(r, LOOP_T0 + j)
                for t in (14, 15, 16):
                    pool_step(0, t)

            def pool_batch(b, more):
                for f in range(FC):
                    n = FC * b + f
                    if more and f % 4 == 0:
                        mlp_rows(b + 1, f // 4, 0)
                    wait_past(pool, s_fc2, n - 1)
                    pool.wait_ge(s_gelu, n + 1)
                    alone(pool, s_passed[0])
                    g.tensor_scalar(gh[:, f % 2, 0], g32[:, f % 2], up[:, UP_G:UP_G + 1], 1.0,
                                    ALU.mult, ALU.mult).then_inc(s_ghi, 1)
                    if isinstance(b, int) and b == 0 and f + MLP_AHEAD < 2 * FC:
                        for k in late_blocks(f):
                            mlp_split(k)
                    if more and f % 4 >= 2:
                        mlp_rows(b + 1, f // 4, f % 4)

            pool_batch(0, True)
            with pool.Fori(1, B - 1) as b:
                pool_batch(b, True)
            pool_batch(B - 1, False)

        @block.scalar
        def _(act):
            a = nc.scalar
            act.wait_ge(s_vec, 16)
            act.wait_ge(s_up, 1)

            def head_kv(l, phase, h, slot):
                u = prep_use(l, phase, h)
                act.wait_ge(s_kv_mm, u + 1)
                wait_past(act, s_prep_mm, u - 1)
                if phase == 0:
                    o = l * V_LAYER + V_BQ
                    a.activation(bq_now[:, slot:slot + 1], col(vec[:, o:o + H], h), ACT.Copy)
                a.activation(kv[:, slot], ptp[:, slot * BLK:slot * BLK + BS], ACT.Identity,
                             bias=col(kvb[:, l, phase], h)).then_inc(s_kv, 1)

            def col(v, h):
                return v[:, bass.ds(h, 1)]

            def head_m(l, h, slot):
                n = H * l + h
                act.wait_ge(s_qkb_mm, n + 1)
                a.activation(qk_bias[:].rearrange("p (b n) -> p b n", b=B)[:, :, bass.ds(h * S, S)],
                             acc[:, 0:BS].rearrange("p (b s) -> p b s", b=B), ACT.Copy,
                             scale=QK_SCALE).then_inc(s_qkb, 1)
                act.wait_ge(s_prep_mm, prep_use(l, 0, h) + 1)
                a.activation(m_out[:, :, :, bass.ds(h * S, S)],
                             pairs[slot][:].rearrange("p (c b s) -> p c b s", c=C, b=B),
                             ACT.Copy).then_inc(s_prep, 1)

            def head_vw(l, h, hh, slot):
                act.wait_ge(s_prep_mm, prep_use(l, 1, h) + 1)
                for par in range(2):
                    src = pairs[slot][S * par:S * (par + 1), :].rearrange("p (g n) -> p g n", g=2)
                    last = a.activation(vw_out[S * slot:S * (slot + 1), par::2, hh, :], src, ACT.Copy)
                last.then_inc(s_prep, 1)

            def affine(n, vector):
                act.wait_ge(s_nt, n + 1)
                for c in range(C):
                    last = a.activation(xh[:, c * P:(c + 1) * P], ntp[:, c * P:(c + 1) * P], ACT.Identity,
                                        scale=lnv[:, vector, c:c + 1], bias=lnv[:, vector, C + c:C + c + 1])
                last.then_inc(s_h32, 1)

            def look_at(l, n):
                if l:
                    return
                wait_past(act, s_wm, 16 * n)
                at = (SPARE + MB) * BLK + n * (WB * BLK)
                src = w12_d[:, bass.ds(n * (WB * BLK), WB * BLK)]
                act.dma_start(store[:, bass.ds(at, WB * BLK)], src).then_inc(s_wm, 16)

            for l in range(LAYERS):
                base = NT_ALL * l
                head_kv(l, 0, 0, 0)
                for h in range(2):
                    head_kv(l, 0, h + 1, (h + 1) % 2)
                    head_m(l, h, h % 2)
                look_at(l, 0)
                with act.Fori(1, H // 2 - 1) as r:
                    for j in range(2):
                        head_kv(l, 0, 2 * r + j + 1, (j + 1) % 2)
                        head_m(l, 2 * r + j, j)
                    look_at(l, r)
                head_kv(l, 0, H - 1, 1)
                head_m(l, H - 2, 0)
                look_at(l, H // 2 - 1)
                head_kv(l, 1, 0, 0)
                head_m(l, H - 1, 1)
                if l == 0:
                    act.wait_ge(s_wm_mag, 2 * WPARTS)
                with act.Fori(0, H // 2 - 1) as r:
                    for j in range(2):
                        head_kv(l, 1, 2 * r + j + 1, (j + 1) % 2)
                        head_vw(l, 2 * r + j, r, j)
                affine(base, l)
                head_kv(l, 1, H - 1, 1)
                head_vw(l, H - 2, H // 2 - 1, 0)
                head_vw(l, H - 1, H // 2 - 1, 1)
                act.wait_ge(s_crow_mm, l + 1)
                a.activation(crow[:], acc[:], ACT.Copy).then_inc(s_crow_ok, 1)

                def act_step(r, t):
                    if t >= 1:
                        n = base + 4 * r + t - 1
                        for k in range(2):
                            act.wait_ge(s_tp, 2 * n + k + 1)
                            wait_past(act, s_pv, n)
                            a.activation(pt[:, 0, k * BLK:(k + 1) * BLK], ptp[:, k * BLK:(k + 1) * BLK],
                                         ACT.Copy).then_inc(s_pt_hi, 1)
                    if t + 2 < NT_ALL:
                        affine(base + 4 * r + t + 2, l)
                    for q in early_rows(l, t)[:1]:
                        affine(NT_ALL * LAYERS + q, LAYERS)
                    if t + 1 < NT_ALL:
                        n = base + 4 * r + t + 1
                        slot = (t + 1) % 2
                        act.wait_ge(s_top, n + 1)
                        a.activation(etop[:, slot], top[:, slot], ACT.Exp, scale=-1.0).then_inc(s_etop, 1)
                        act.wait_ge(s_sub, n + 1)
                        a.activation(ls[slot], ls[slot], ACT.Exp).then_inc(s_exp, 1)
                    for q in early_rows(l, t)[1:]:
                        affine(NT_ALL * LAYERS + q, LAYERS)

                for t in (-1, 0, 1):
                    act_step(0, t)
                with act.Fori(0, LOOP_STEPS // 4) as r:
                    for j in range(4):
                        act_step(r, LOOP_T0 + j)
                for t in (14, 15, 16):
                    act_step(0, t)

            base = NT_ALL * LAYERS

            def act_batch(b, more):
                for f in range(FC):
                    n = FC * b + f
                    if more and f % 4 == 2:
                        affine(base + TPB * (b + 1) + f // 4, LAYERS)
                    act.wait_ge(s_fc1, n + 1)
                    wait_past(act, s_g, n - 1)
                    o = V_MLP + 2 * C + f
                    a.activation(g32[:, f % 2], ptp[:, (f % 2) * BLK:(f % 2 + 1) * BLK], ACT.Gelu,
                                 scale=dn[:, DN_F1:DN_F1 + 1], bias=vec[:, o:o + 1]).then_inc(s_gelu, 1)

            act_batch(0, True)
            with act.Fori(1, B - 1) as b:
                act_batch(b, True)
            act_batch(B - 1, False)

        @block.vector
        def _(dve):
            v = nc.vector
            chained = [0]

            def link(instruction):
                chained[0] += 1
                instruction.then_inc(s_dve, 1)
                dve.wait_ge(s_dve, chained[0])

            def power(src, at, n=1):
                p_ap = dn[:, at:at + n]
                link(v.tensor_scalar(p_ap.bitcast(U32), src.bitcast(U32), EXP_MASK, None, ALU.bitwise_and))
                link(v.tensor_scalar(p_ap, p_ap, 2.0 ** -80, None, ALU.max))
                link(v.reciprocal(up[:, at:at + n], p_ap))
                link(v.tensor_scalar(up[:, at:at + n], up[:, at:at + n], TOP, None, ALU.mult))
                return v.tensor_scalar(p_ap, p_ap, 1.0 / TOP, None, ALU.mult)

            dve.wait_ge(s_vec, 16)
            for l in range(LAYERS):
                o = l * V_LAYER
                v.tensor_tensor(kvb[:, l], vec[:, o + V_BK:o + V_BK + 2 * H].rearrange("p (a h) -> p a h", a=2),
                                vec[:, o + V_BIASK:o + V_BIASK + 2 * H].rearrange("p (a h) -> p a h", a=2),
                                ALU.subtract)
            ln_at = [V_LNS, V_LAYER + V_LNS, V_MLP]
            for n, o in enumerate(ln_at):
                last = v.tensor_reduce(lm[:, 2 * n:2 * n + 2], vec[:, o:o + 2 * C].rearrange("p (a c) -> p a c", a=2),
                                       AX.X, ALU.max, apply_absolute_value=True)
            last.then_inc(s_lm, 1)
            dve.wait_ge(s_gm, 1)
            for n in range(LAYERS + 1):
                last = v.scalar_tensor_tensor(bound[:, n:n + 1], gm[:, 2 * n:2 * n + 1], LN_MAX,
                                              gm[:, 2 * n + 1:2 * n + 2], ALU.mult, ALU.add)
            link(last)
            link(power(bound[:, 0:3], UP_LN, 3))
            for n, o in enumerate(ln_at):
                last = v.tensor_scalar(lnv[:, n], vec[:, o:o + 2 * C], up[:, UP_LN + n:UP_LN + n + 1], None, ALU.mult)
            last.then_inc(s_up, 1)

            def split_lo(count, slot, col):
                dve.wait_ge(s_hi, count + 1)
                v.scalar_tensor_tensor(halves[:, bass.ds(slot * 2 * BLK + BLK, BLK)],
                                       store[:, bass.ds((slot + SPARE) * BLK, BLK)], up[:, col:col + 1],
                                       halves[:, bass.ds(slot * 2 * BLK, BLK)],
                                       ALU.mult, ALU.subtract).then_inc(s_lo, 1)

            def mlp_split(k):
                landed, slot, col = mlp_block(k)
                dve.wait_ge(landed, 16)
                split_lo(split_base(LAYERS, 0) + k, slot, col)

            def row_stats(n, tile, loaded=None):
                if loaded is not None:
                    dve.wait_ge(loaded, 16)
                else:
                    dve.wait_ge(s_xr, n - NT_ALL + 1)
                v.bn_stats(stats[:], x[:, bass.ds(tile, 1), :].squeeze(1)).then_inc(s_bn, 1)
                dve.wait_ge(s_bn, n + 1)
                alone(dve, s_passed[1])
                v.bn_aggr(mv[:], stats[:]).then_inc(s_mv, 1)

            def norm_rows(n, tile):
                dve.wait_ge(s_rstd, n + 1)
                wait_past(dve, s_h, n)
                v.tensor_scalar(xh[:], x[:, bass.ds(tile, 1), :].squeeze(1), mv[:, 0:1], rstd[:, 0:1], ALU.subtract,
                                ALU.mult).then_inc(s_xh, 1)

            def look_at(n):
                dve.wait_ge(s_wm, 16 * (n + 1))
                v.tensor_reduce(mw[:, bass.ds(n, 1)], store[:, bass.ds((SPARE + MB) * BLK + n * (WB * BLK), WB * BLK)],
                                AX.X, ALU.max, apply_absolute_value=True).then_inc(s_wm_mag, 1)

            def head_mag(l, h):
                dve.wait_ge(s_prep, prep_use(l, 0, h) + 1)
                v.tensor_reduce(mx[:, 0, bass.ds(h, 1)], m_cols[:, :, bass.ds(h * S, S)], AX.XY, ALU.max,
                                apply_absolute_value=True).then_inc(s_mag, 1)

            for l in range(LAYERS):
                base = NT_ALL * l
                mags = (H + J) * l
                if l == 0:
                    for h in range(2):
                        head_mag(l, h)
                    with dve.Fori(1, H // 2) as r:
                        look_at(r - 1)
                        for j in range(2):
                            head_mag(l, 2 * r + j)
                    look_at(H // 2 - 1)
                    dve.wait_ge(s_wm_mag, 2 * WPARTS)
                    v.tensor_reduce(lm[:, 1:2], mw[:, 0:WPARTS], AX.X, ALU.max)
                    v.tensor_reduce(lm[:, 2:3], vec[:, V_MLP + 2 * C:V_ALL], AX.X, ALU.max, apply_absolute_value=True)
                    v.tensor_reduce(lm[:, 3:4], mw[:, WPARTS:2 * WPARTS], AX.X, ALU.max)
                else:
                    with dve.Fori(0, H) as h:
                        head_mag(l, h)
                dve.wait_ge(s_mag, mags + H)
                v.tensor_reduce(lm[:, 0:1], mx[:, 0, :], AX.X, ALU.max).then_inc(s_lm, 1)
                dve.wait_ge(s_gm, 2 + 2 * l)
                if l == 0:
                    link(power(gm[:, 1:2], UP_W1))
                    link(power(gm[:, 3:4], UP_W2))
                    link(v.tensor_scalar(bound[:, 3:4], gm[:, 1:2], bound[:, 2:3], float(D), ALU.mult, ALU.mult))
                    link(v.tensor_tensor(bound[:, 3:4], bound[:, 3:4], gm[:, 2:3], ALU.add))
                    link(power(bound[:, 3:4], UP_G))
                    link(v.tensor_tensor(dn[:, DN_F1:DN_F1 + 1], dn[:, UP_W1:UP_W1 + 1],
                                         dn[:, UP_LN + LAYERS:UP_LN + LAYERS + 1], ALU.mult))
                    link(v.tensor_tensor(dn[:, DN_F2:DN_F2 + 1], dn[:, UP_W2:UP_W2 + 1], dn[:, UP_G:UP_G + 1],
                                         ALU.mult))
                link(power(gm[:, 0:1], UP_M))
                link(v.tensor_scalar(dn[:, DN_L:DN_L + 1], dn[:, UP_M:UP_M + 1], dn[:, UP_LN + l:UP_LN + l + 1],
                                     QK_SCALE, ALU.mult, ALU.mult))
                v.tensor_scalar(dn[:, DN_L:DN_L + 1], dn[:, DN_L:DN_L + 1], 1.0, None,
                                ALU.mult).then_inc(s_up, 1)
                dve.wait_ge(s_row, 16 * (l + 1))

                def v_heads(r, e):
                    for j in range(2):
                        dve.wait_ge(s_ring_b[j], 16 * (H * l + H // 2 + r + 1))
                        wait_past(dve, s_crow, H * l + 2 * r + j)
                        o = l * V_LAYER + V_BIASV
                        v.scalar_tensor_tensor(crow[:], ring[j][:, D:2 * D], vec[:, bass.ds(2 * r + (o + j), 1)],
                                               crow[:], ALU.mult, ALU.add).then_inc(s_crow, 1)
                        for k in range(2):
                            split_lo(split_base(l, 0) + 4 * r + 2 * j + k, 4 * r + 2 * j + k, UP_M)
                    dve.wait_ge(s_prep, prep_use(l, 1, 2 * r + 1) + 1)
                    v.tensor_reduce(mx[:, 1, bass.ds(r, 1)], vw_out[:, :, r, :], AX.XY, ALU.max,
                                    apply_absolute_value=True).then_inc(s_mag, 1)

                if l == 0:
                    v_heads(0, 0)
                    with dve.Fori(1, H // 2 - 1) as r:
                        v_heads(r, r)
                else:
                    with dve.Fori(0, H // 2 - 1) as r:
                        v_heads(r, r)
                row_stats(base, 0, s_x[0] if l == 0 else None)
                norm_rows(base, 0)
                v_heads(H // 2 - 1, 0)
                row_stats(base + 1, 1, s_x[0] if l == 0 else None)
                norm_rows(base + 1, 1)
                dve.wait_ge(s_mag, mags + H + J)
                v.tensor_reduce(lm[:, 0:1], mx[:, 1, 0:J], AX.X, ALU.max).then_inc(s_lm, 1)
                dve.wait_ge(s_gm, 3 + 2 * l)
                link(power(gm[:, 0:1], UP_VW))
                v.tensor_scalar(dn[:, DN_VW:DN_VW + 1], dn[:, UP_VW:UP_VW + 1], 1.0 / TOP, None,
                                ALU.mult).then_inc(s_up, 1)
                for k in range(MB, MB + J):
                    split_lo(split_base(l, 0) + k, k, UP_VW)
                if l == 0:
                    for b in range(1, B):
                        dve.wait_ge(s_x[b], 16)

                def dve_step(r, t):
                    if t >= 1:
                        n = base + 4 * r + t - 1
                        for k in range(2):
                            dve.wait_ge(s_pt_hi, 2 * n + k + 1)
                            v.tensor_tensor(pt[:, 1, k * BLK:(k + 1) * BLK], ptp[:, k * BLK:(k + 1) * BLK],
                                            pt[:, 0, k * BLK:(k + 1) * BLK], ALU.subtract).then_inc(s_pt, 1)
                    rows = [(NT_ALL * LAYERS + q, q) for q in early_rows(l, t)]
                    if t + 2 < NT_ALL:
                        rows = [(base + 4 * r + t + 2, 4 * r + t + 2)]
                    if t >= 0 and rows:
                        row_stats(*rows[0], s_x[0] if l == 0 else None)
                    if LOOP_T0 <= t < LOOP_T0 + LOOP_STEPS:
                        for k in range(2):
                            split_lo(split_base(l, 0) + MB + J + 8 * r + 2 * (t - LOOP_T0) + k, MB + J + 8 * r + 2 * (t - LOOP_T0) + k, UP_VW)
                    if t >= 0 and rows:
                        norm_rows(*rows[0])
                    slot = (t + 1) % 2
                    tops = top[:, slot].unsqueeze(2).to_broadcast([P, H, S])
                    if t + 1 < NT_ALL:
                        n = base + 4 * r + t + 1
                        heads = ls[slot].rearrange("p (h s) -> p h s", h=H)
                        b = r + (t + 1) // 4
                        dve.wait_ge(s_L, n + 1)
                        wait_past(dve, s_tp, 2 * (n - 1))
                        dve.wait_ge(s_qkb, H * (l + 1))
                        v.scalar_tensor_tensor(ls[slot], pairs[slot][:], dn[:, DN_L:DN_L + 1],
                                               qk_bias[:, bass.ds(b * HS, HS)], ALU.mult, ALU.add).then_inc(s_ls, 1)
                        dve.wait_ge(s_ls, n + 1)
                        v.tensor_reduce(top[:, slot], heads, AX.X, ALU.max).then_inc(s_top0, 1)
                        dve.wait_ge(s_top0, n + 1)
                        v.tensor_scalar(top[:, slot], top[:, slot], 0.0, None, ALU.max).then_inc(s_top, 1)
                        dve.wait_ge(s_top, n + 1)
                        v.tensor_tensor(heads, heads, tops, ALU.subtract).then_inc(s_sub, 1)
                    if t + 1 < NT_ALL:
                        n = base + 4 * r + t + 1
                        dve.wait_ge(s_exp, n + 1)
                        v.tensor_reduce(tot[:, slot], ls[slot].rearrange("p (h s) -> p h s", h=H), AX.X,
                                        ALU.add).then_inc(s_sum, 1)
                        dve.wait_ge(s_sum, n + 1)
                        dve.wait_ge(s_etop, n + 1)
                        v.tensor_tensor(tot[:, slot], tot[:, slot], etop[:, slot], ALU.add).then_inc(s_tot, 1)
                        dve.wait_ge(s_tot, n + 1)
                        v.tensor_scalar(tot[:, slot], tot[:, slot], 1.0 / TOP, None, ALU.mult).then_inc(s_tot2, 1)
                        dve.wait_ge(s_tot2, n + 1)
                        v.reciprocal(tot[:, slot], tot[:, slot]).then_inc(s_rc, 1)
                    for k in early_blocks(l, t):
                        mlp_split(k)
                    for row in rows[1:]:
                        row_stats(*row)
                        norm_rows(*row)
                    if t >= 1:
                        m = base + 4 * r + t - 1
                        i = 4 * r + t - 1
                        dve.wait_ge(s_pv, m + 1)
                        dve.wait_ge(s_xc, m + 1)
                        v.scalar_tensor_tensor(x[:, bass.ds(i, 1), :].squeeze(1), acc[:], dn[:, DN_VW:DN_VW + 1], x[:, bass.ds(i, 1), :].squeeze(1),
                                               ALU.mult, ALU.add).then_inc(s_xr, 1)

                for t in (-1, 0, 1):
                    dve_step(0, t)
                with dve.Fori(0, LOOP_STEPS // 4) as r:
                    for j in range(4):
                        dve_step(r, LOOP_T0 + j)
                for t in (14, 15, 16):
                    dve_step(0, t)

            base = NT_ALL * LAYERS

            def dve_batch(b, more):
                for f in range(FC):
                    n = FC * b + f
                    row = (base + TPB * (b + 1) + f // 4, TPB * (b + 1) + f // 4)
                    if more and f % 4 == 0:
                        row_stats(*row)
                    dve.wait_ge(s_ghi, n + 1)
                    v.scalar_tensor_tensor(gh[:, f % 2, 1], g32[:, f % 2], up[:, UP_G:UP_G + 1], gh[:, f % 2, 0],
                                           ALU.mult, ALU.subtract).then_inc(s_g, 1)
                    if isinstance(b, int) and b == 0:
                        for k in late_blocks(f):
                            mlp_split(k)
                    if more and f % 4 == 0:
                        norm_rows(*row)
                for q in range(TPB):
                    i = TPB * b + q
                    dve.wait_ge(s_fc2, FC * (b + 1))
                    dve.wait_ge(s_xc, base + i + 1)
                    v.scalar_tensor_tensor(x[:, bass.ds(i, 1), :].squeeze(1), pairs[q // 2][:, (q % 2) * BLK:(q % 2 + 1) * BLK],
                                           dn[:, DN_F2:DN_F2 + 1], x[:, bass.ds(i, 1), :].squeeze(1), ALU.mult, ALU.add).then_inc(s_y, 1)

            dve_batch(0, True)
            with dve.Fori(1, B - 1) as b:
                dve_batch(b, True)
            dve_batch(B - 1, False)

        @block.tensor
        def _(pe):
            t_ = nc.tensor

            def head_kv(l, phase, h, slot, slot_uses):
                u = prep_use(l, phase, h)
                pe.wait_ge(s_ring_a[slot], 16 * slot_uses)
                wait_past(pe, s_kv, u - 1)
                for c in range(C):
                    last = t_.matmul(ptp[:, slot * BLK:slot * BLK + BS], ring[slot][:, c * P:(c + 1) * P],
                                     cT[:, c, :], start=(c == 0), stop=(c == C - 1))
                last.then_inc(s_kv_mm, 1)

            def head_m(l, h, slot, slot_uses):
                u = prep_use(l, 0, h)
                pe.wait_ge(s_kv, u + 1)
                wait_past(pe, s_qkb, H * l + h)
                if isinstance(h, int) and h == 0:
                    wait_past(pe, s_xr, NT_ALL * l)
                t_.matmul(acc[:, 0:BS], bq_now[:, slot:slot + 1].to_broadcast([P, P]), kv[:, slot],
                          start=True, stop=True).then_inc(s_qkb_mm, 1)
                wait_past(pe, s_prep, u - 1)
                pe.wait_ge(s_ring_b[slot], 16 * slot_uses)
                for c in range(C):
                    last = t_.matmul(pairs[slot][:, c * BS:(c + 1) * BS], ring[slot][:, D + c * P:D + (c + 1) * P],
                                     kv[:, slot], start=True, stop=True)
                last.then_inc(s_prep_mm, 1)

            def head_vw(l, h, slot, slot_uses):
                u = prep_use(l, 1, h)
                pe.wait_ge(s_kv, u + 1)
                pe.wait_ge(s_prep, u - 1)
                pe.wait_ge(s_ring_b[slot], 16 * slot_uses)
                for g in range(2):
                    last = t_.matmul(pairs[slot][:, g * BLK:(g + 1) * BLK], kv[:, slot, g * P:(g + 1) * P],
                                     ring[slot][:, D:2 * D], start=True, stop=True)
                last.then_inc(s_prep_mm, 1)

            def transposes(n):
                pe.wait_ge(s_xh, n + 1)
                wait_past(pe, s_h32, n)
                for c in range(C):
                    last = t_.transpose(ntp[:, c * P:(c + 1) * P], xh[:, c * P:(c + 1) * P], ident[:])
                last.then_inc(s_nt, 1)

            pe.wait_ge(s_const, 1)
            for l in range(LAYERS):
                base = NT_ALL * l
                uses = H * l
                pe.wait_ge(s_ctx, 16 * (l + 1))
                head_kv(l, 0, 0, 0, uses + 1)
                for h in range(2):
                    head_kv(l, 0, h + 1, (h + 1) % 2, uses + (h + 1) // 2 + 1)
                    head_m(l, h, h % 2, uses + 1)
                with pe.Fori(1, H // 2 - 1) as r:
                    for j in range(2):
                        head_kv(l, 0, 2 * r + j + 1, (j + 1) % 2, uses + r + (j + 1) // 2 + 1)
                        head_m(l, 2 * r + j, j, uses + r + 1)
                head_kv(l, 0, H - 1, 1, uses + H // 2)
                head_m(l, H - 2, 0, uses + H // 2)
                head_kv(l, 1, 0, 0, uses + H // 2 + 1)
                head_m(l, H - 1, 1, uses + H // 2)
                with pe.Fori(0, H // 2 - 1) as r:
                    for j in range(2):
                        head_kv(l, 1, 2 * r + j + 1, (j + 1) % 2, uses + H // 2 + r + (j + 1) // 2 + 1)
                        head_vw(l, 2 * r + j, j, uses + H // 2 + r + 1)
                transposes(base)
                head_kv(l, 1, H - 1, 1, uses + H)
                head_vw(l, H - 2, 0, uses + H)
                head_vw(l, H - 1, 1, uses + H)
                pe.wait_ge(s_crow, H * (l + 1))
                pe.wait_ge(s_qkb, H * (l + 1))
                t_.matmul(acc[:], ones[:], crow[:], start=True, stop=True).then_inc(s_crow_mm, 1)
                pe.wait_ge(s_prep, prep_use(l + 1, 0, 0))

                def pe_step(r, t):
                    if t >= 1:
                        n = base + 4 * r + t - 1
                        pe.wait_ge(s_prob, n + 1)
                        wait_past(pe, s_pt, 2 * n)
                        for j in range(J):
                            tr = t_.transpose(ptp[:, j * P:(j + 1) * P], ls[(t - 1) % 2][:, j * P:(j + 1) * P], ident[:])
                            if j % 4 == 3:
                                tr.then_inc(s_tp, 1)
                    if t + 1 < NT_ALL:
                        n = base + 4 * r + t + 1
                        slot = (t + 1) % 2
                        b = r + (t + 1) // 4
                        pe.wait_ge(s_h, n + 1)
                        pe.wait_ge(s_lo, split_base(l, 0) + 2 * C * (b + 1))
                        wait_past(pe, s_ls, n - 1)
                        for c in range(C):
                            for half, mhalf in ((0, 0), (0, 1), (1, 0)):
                                for g in range(2):
                                    at = (b * 2 * C + 2 * c + g) * 2 * BLK + mhalf * BLK
                                    last = t_.matmul(pairs[slot][:, g * BLK:(g + 1) * BLK], hT[:, slot, half, c, :],
                                                     halves[:, bass.ds(at, BLK)], start=(c == 0 and half + mhalf == 0),
                                                     stop=(c == C - 1 and half == 1))
                        last.then_inc(s_L, 1)
                    if t + 2 < NT_ALL:
                        transposes(base + 4 * r + t + 2)
                    for q in early_rows(l, t)[:1]:
                        transposes(NT_ALL * LAYERS + q)
                    if t >= 1:
                        n = base + 4 * r + t - 1
                        b = r + (t - 1) // 4
                        pe.wait_ge(s_pt, 2 * n + 2)
                        pe.wait_ge(s_lo, split_base(l, 1) + J * (b + 1))
                        pe.wait_ge(s_crow_ok, l + 1)
                        wait_past(pe, s_xr, n)
                        for j in range(J):
                            for half, vhalf in ((0, 0), (0, 1), (1, 0)):
                                at = (MB + b * J + j) * 2 * BLK + vhalf * BLK
                                last = t_.matmul(acc[:], pt[:, half, j * P:(j + 1) * P], halves[:, bass.ds(at, BLK)],
                                                 start=(j == 0 and half + vhalf == 0), stop=(j == J - 1 and half == 1))
                        last.then_inc(s_pv, 1)
                    for q in early_rows(l, t)[1:]:
                        transposes(NT_ALL * LAYERS + q)

                for t in (-1, 0, 1):
                    pe_step(0, t)
                with pe.Fori(0, LOOP_STEPS // 4) as r:
                    for j in range(4):
                        pe_step(r, LOOP_T0 + j)
                for t in (14, 15, 16):
                    pe_step(0, t)

            base = NT_ALL * LAYERS

            def fc1(b, f):
                n = FC * b + f
                wait_past(pe, s_gelu, n - 1)
                pe.wait_ge(s_lo, split_base(LAYERS, 0) + f + 1)
                pe.wait_ge(s_h, base + TPB * (b + 1))
                for c in range(C):
                    for whalf, half in ((0, 0), (0, 1), (1, 0)):
                        at = (f * 2 + whalf) * BLK + c * P
                        src = mlp_rows_at(b, half)[:, c, :]
                        last = t_.matmul(ptp[:, (f % 2) * BLK:(f % 2 + 1) * BLK], halves[:, at:at + P], src,
                                         start=(c == 0 and whalf + half == 0), stop=(c == C - 1 and whalf == 1))
                last.then_inc(s_fc1, 1)

            def fc2(b, f):
                n = FC * b + f
                pe.wait_ge(s_g, n + 1)
                pe.wait_ge(s_lo, split_base(LAYERS, 0) + FC + f + 1)
                if f == 0:
                    wait_past(pe, s_y, TPB * b)
                for q in range(TPB):
                    for half, whalf in ((0, 0), (0, 1), (1, 0)):
                        at = ((W2_AT + f) * 2 + whalf) * BLK
                        last = t_.matmul(pairs[q // 2][:, (q % 2) * BLK:(q % 2 + 1) * BLK],
                                         gh[:, f % 2, half, q * P:(q + 1) * P], halves[:, bass.ds(at, BLK)],
                                         start=(f == 0 and half + whalf == 0), stop=(f == FC - 1 and half == 1))
                last.then_inc(s_fc2, 1)

            def pe_batch(b, more):
                fc1(b, 0)
                for f in range(FC):
                    if f + 1 < FC:
                        fc1(b, f + 1)
                    if more and f % 4 == 1:
                        transposes(base + TPB * (b + 1) + f // 4)
                    fc2(b, f)

            pe_batch(0, True)
            with pe.Fori(1, B - 1) as b:
                pe_batch(b, True)
            pe_batch(B - 1, False)


def kernel(**inputs):
    import numpy as np
    import concourse.bacc as bacc
    from concourse.bass_utils import run_bass_kernel_spmd

    w = {k.replace("L0_xattn_", ""): np.asarray(v) for k, v in inputs.items()}

    def by_chunk(v):
        return v.reshape(-1, P).T

    def heads_in(m):
        return m.reshape(C, P, H, K).transpose(2, 1, 0, 3).reshape(H, P, C * K)

    weights = np.stack([np.concatenate([
        np.concatenate([heads_in(w[f"wk{i}"]), w[f"wq{i}"].T.reshape(H, K, D)], axis=2),
        np.concatenate([heads_in(w[f"wv{i}"]), w[f"wo{i}"].reshape(H, K, D)], axis=2)]) for i in (1, 2)])
    cols = []
    for i in (1, 2):
        for name in (f"bq{i}", f"bk{i}", f"bv{i}", f"bias_k{i}", f"bias_v{i}", f"ln{i}_scale", f"ln{i}_offset"):
            cols.append(by_chunk(w[name].reshape(-1)))
    for name in ("ln_mlp_scale", "ln_mlp_offset", "b_fc1"):
        cols.append(by_chunk(w[name]))
    arrays = {
        "x": w["x"].reshape(B * Q, D),
        "ctxT": w["ctx_2048"].reshape(BS, C, P).transpose(2, 1, 0).reshape(P, C * BS),
        "weights": weights,
        "vectors": np.concatenate(cols, axis=1),
        "rows": np.stack([w["bo1"], w["bo2"], w["b_fc2"]]),
        "w12": np.concatenate([w["w_fc1"].reshape(C, P, FC, P).transpose(1, 2, 0, 3).reshape(P, FC * D),
                               w["w_fc2"].reshape(FC, P, D).transpose(1, 0, 2).reshape(P, FC * D)], axis=1),
    }
    arrays = {k: np.ascontiguousarray(v) for k, v in arrays.items()}
    nc = bacc.Bacc("TRN2", target_bir_lowering=False, num_devices=1)
    args = [nc.dram_tensor(k + "_dram", v.shape, F32, kind="ExternalInput").ap() for k, v in arrays.items()]
    args.append(nc.dram_tensor("y_dram", (B * Q, D), F32, kind="ExternalOutput").ap())
    program(nc, *args)
    r = run_bass_kernel_spmd(nc, [{k + "_dram": v for k, v in arrays.items()}], core_ids=[0])
    return np.asarray(r.results[0]["y_dram"]).reshape(B, Q, D)
```

```python
import concourse.bass as bass
from concourse import mybir
from contextlib import ExitStack

F32 = mybir.dt.float32
F16 = mybir.dt.float16
U32 = mybir.dt.uint32
ALU = mybir.AluOpType
ACT = mybir.ActivationFunctionType
AX = mybir.AxisListType
RMAX = bass.bass_isa.ReduceOp.max

P = 128
B, Q, S, D, H, K, F = 4, 512, 64, 512, 16, 128, 2048
LAYERS = 2
C = D // P
TPB = Q // P
NT_ALL = B * TPB
HS = H * S
BS = B * S
J = HS // P
FC = F // P
BLK = 512
MB = B * C * HS // BLK
SPARE = 2
WPARTS = 4
WB = FC // WPARTS
LOOK = FC * D // (H // 2)
W2_AT = MB + 6
EPS = 1e-5
QK_SCALE = float(K) ** -0.5
TOP = 2.0 ** 14
LN_MAX = 23.0
EXP_MASK = 0x7F800000
MLP_AHEAD = 3
V_BQ, V_BK, V_BV, V_BIASK, V_BIASV, V_LNS, V_LNO = 0, H, 2 * H, 3 * H, 4 * H, 5 * H, 5 * H + C
V_LAYER = 5 * H + 2 * C
V_MLP = LAYERS * V_LAYER
V_ALL = V_MLP + 2 * C + FC


def wait_past(eng, sem, count):
    if not isinstance(count, int) or count > 0:
        eng.wait_ge(sem, count)


def alone(eng, passed):
    eng.sem_inc(passed, 1)


def program(nc, x_d, ctx_d, w_d, vec_d, rows_d, w12_d, y_d):
    with ExitStack() as ctx:
        def sb(name, shape, dt=F32):
            return ctx.enter_context(nc.sbuf_tensor(name, shape, dt))

        def sem(name):
            return ctx.enter_context(nc.semaphore(name))

        store = sb("store", [P, (2 * MB + SPARE) * BLK])
        x = sb("x", [P, NT_ALL, D])
        qk_bias = sb("qk_bias", [P, B * HS])
        ring_or_ls = sb("ring_or_ls", [P, 2, 2 * D])
        ctx_or_pt = sb("ctx_or_pt", [P, C * BS])
        kv_or_ph = sb("kv_or_ph", [P, HS])
        hT = sb("hT", [P, 2, 2, C, P], F16)
        xh = sb("xh", [P, D])
        crow = sb("crow", [P, D])
        ident = sb("ident", [P, P])
        ident16 = sb("ident16", [P, P], F16)
        ones = sb("ones", [P, P])
        vec = sb("vec", [P, V_ALL])
        kvb = sb("kvb", [P, LAYERS, 2, H])
        bq_now = sb("bq_now", [P, 2])
        lnv = sb("lnv", [P, LAYERS + 1, 2 * C])
        neg_half = sb("neg_half", [P, 1])
        stats = sb("stats", [P, 6])
        mv = sb("mv", [P, 2])
        ve = sb("ve", [P, 1])
        rstd = sb("rstd", [P, 1])
        top = sb("top", [P, 2, H])
        etop = sb("etop", [P, 2, H])
        tot = sb("tot", [P, 2, H])
        mx = sb("mx", [P, 2, H])
        mw = sb("mw", [P, H // 2])
        lm = sb("lm", [P, 8])
        gm = sb("gm", [P, 8])
        up = sb("up", [P, 16])
        dn = sb("dn", [P, 16])
        UP_LN, UP_M, UP_VW, UP_W1, UP_W2, UP_G = 0, 3, 4, 5, 6, 7
        DN_L, DN_VW, DN_F1, DN_F2 = 8, 9, 10, 11
        bound = sb("bound", [P, 4])

        ring = [ring_or_ls[:, s] for s in range(2)]
        ls = [ring_or_ls[:, s] for s in range(2)]
        hT_flat = hT[:].rearrange("p s a c q -> p (s a c q)").bitcast(F32)

        def cT(l, phase):
            flat = hT_flat if l and phase == 0 else ctx_or_pt[:]
            return flat.rearrange("p (c s) -> p c s", c=C)

        kv = kv_or_ph[:, 0:2 * BS].rearrange("p (s n) -> p s n", s=2)
        ph = kv_or_ph[:].bitcast(F16).rearrange("p (a n) -> p a n", a=2)
        pt = ctx_or_pt[:].bitcast(F16).rearrange("p (a n) -> p a n", a=2)
        halves = store[:].bitcast(F16)
        m_out = store[:, SPARE * BLK:(SPARE + MB) * BLK].rearrange("p (b c n) -> p c b n", b=B, c=C)
        m_cols = store[:, SPARE * BLK:(SPARE + MB) * BLK].rearrange("p (g n) -> p g n", g=B * C)
        vw_out = store[:, (SPARE + MB) * BLK:].rearrange("p (b j n) -> p b j n", b=B, j=J)
        g32 = qk_bias[:, 0:2 * Q].rearrange("p (s n) -> p s n", s=2)
        gh = qk_bias[:, 2 * Q:4 * Q].bitcast(F16).rearrange("p (s a n) -> p s a n", s=2, a=2)

        pairs = [ctx.enter_context(nc.psum_tensor(f"pair{s}", [P, 2 * BLK], F32)) for s in range(2)]
        ptp = ctx.enter_context(nc.psum_tensor("ptp", [P, 2 * BLK], F32))
        ptp16 = ptp[:].bitcast(F16).rearrange("p (a n) -> p a n", a=2)
        acc = ctx.enter_context(nc.psum_tensor("acc", [P, BLK], F32))
        ntp = ctx.enter_context(nc.psum_tensor("ntp", [P, BLK], F32))

        s_vec = sem("s_vec")
        s_x = [sem(f"s_x{b}") for b in range(B)]
        s_ctx = sem("s_ctx")
        s_ring_a = [sem(f"s_ring_a{s}") for s in range(2)]
        s_ring_b = [sem(f"s_ring_b{s}") for s in range(2)]
        s_row = sem("s_row")
        s_wm = sem("s_wm")
        s_wm_mag = sem("s_wm_mag")
        s_w1 = [sem(f"s_w1_{n}") for n in range(WPARTS)]
        s_w2 = [sem(f"s_w2_{n}") for n in range(WPARTS)]
        s_out = sem("s_out")
        s_ident0 = sem("s_ident0")
        s_const = sem("s_const")
        s_acc0 = sem("s_acc0")
        s_dve = sem("s_dve")
        s_lm = sem("s_lm")
        s_gm = sem("s_gm")
        s_up = sem("s_up")
        s_kv_mm = sem("s_kv_mm")
        s_kv = sem("s_kv")
        s_qkb_mm = sem("s_qkb_mm")
        s_qkb = sem("s_qkb")
        s_prep_mm = sem("s_prep_mm")
        s_prep = sem("s_prep")
        s_mag = sem("s_mag")
        s_crow = sem("s_crow")
        s_crow_mm = sem("s_crow_mm")
        s_crow_ok = sem("s_crow_ok")
        s_hi = sem("s_hi")
        s_lo = sem("s_lo")
        s_bn = sem("s_bn")
        s_mv = sem("s_mv")
        s_ve = sem("s_ve")
        s_rstd = sem("s_rstd")
        s_xh = sem("s_xh")
        s_nt = sem("s_nt")
        s_h32 = sem("s_h32")
        s_hhi = sem("s_hhi")
        s_h = sem("s_h")
        s_L = sem("s_L")
        s_ls = sem("s_ls")
        s_top0 = sem("s_top0")
        s_top = sem("s_top")
        s_etop = sem("s_etop")
        s_sub = sem("s_sub")
        s_exp = sem("s_exp")
        s_sum = sem("s_sum")
        s_tot = sem("s_tot")
        s_tot2 = sem("s_tot2")
        s_rc = sem("s_rc")
        s_prob = sem("s_prob")
        s_phi = sem("s_phi")
        s_ph = sem("s_ph")
        s_tp = sem("s_tp")
        s_pt = sem("s_pt")
        s_pv = sem("s_pv")
        s_xc = sem("s_xc")
        s_xr = sem("s_xr")
        s_fc1 = sem("s_fc1")
        s_gelu = sem("s_gelu")
        s_ghi = sem("s_ghi")
        s_g = sem("s_g")
        s_fc2 = sem("s_fc2")
        s_fc2_tile = sem("s_fc2_tile")
        s_y = sem("s_y")

        s_passed = [sem(f"s_passed{e}") for e in range(3)]

        block = ctx.enter_context(nc.Block())

        def prep_use(l, phase, h):
            return 2 * H * l + H * phase + h

        def split_base(l, what):
            return 2 * MB * l + MB * what

        LOOP_T0, LOOP_STEPS = 2, NT_ALL - 4

        def vw_blocks(t):
            return {2: (0, 1), 3: (2, 3), 4: (4, 5), 5: (6, 7)}.get(t, ())

        def mlp_rows_at(b, half):
            slot = MB if isinstance(b, int) and b == 0 else FC + C * b
            at = (2 * slot + C * half) * BLK
            return halves[:, bass.ds(at, C * Q)].rearrange("p (c t) -> p c t", c=C)

        def mlp_dst(b, half, q):
            return mlp_rows_at(b, half)[:, :, q * P:(q + 1) * P]

        def mlp_block(k):
            f = k // 2
            if k % 2 == 0:
                return s_w1[f // WB], f, UP_W1
            return s_w2[f // WB], W2_AT + f, UP_W2

        def late_blocks(f):
            return range(2 * (f + MLP_AHEAD), min(2 * (f + MLP_AHEAD + 1), 2 * FC))

        @block.sync
        def _(sp):
            sp.dma_start(vec[:], vec_d).then_inc(s_vec, 16)
            sp.dma_start(ctx_or_pt[:], ctx_d).then_inc(s_ctx, 16)
            x_v = x_d.rearrange("(i p) d -> p i d", p=P)
            y_v = y_d.rearrange("(i p) d -> p i d", p=P)

            def load_x(b):
                sp.dma_start(x[:, b * TPB:(b + 1) * TPB, :], x_v[:, b * TPB:(b + 1) * TPB, :]).then_inc(s_x[b], 16)

            def load_a(l, u, slot):
                wait_past(sp, s_kv_mm, 2 * H * l + u - 1)
                alone(sp, s_passed[2])
                sp.dma_start(ring[slot][:, 0:D], w_d[l, u][:, 0:D]).then_inc(s_ring_a[slot], 16)

            def load_b(l, u, slot, crow_too):
                if crow_too:
                    sp.wait_ge(s_crow, H * l + u - H - 1)
                    alone(sp, s_passed[2])
                else:
                    wait_past(sp, s_mag, 2 * H * l + u - 1)
                    alone(sp, s_passed[2])
                wait_past(sp, s_prep_mm, 2 * H * l + u - 1)
                alone(sp, s_passed[2])
                sp.dma_start(ring[slot][:, D:2 * D], w_d[l, u][:, D:2 * D]).then_inc(s_ring_b[slot], 16)

            for l in range(LAYERS):
                if l:
                    sp.wait_ge(s_L, NT_ALL * l)
                    sp.dma_start(hT_flat, ctx_d).then_inc(s_ctx, 16)
                    sp.wait_ge(s_ph, NT_ALL * l - 1)
                    load_a(l, 0, 0)
                    sp.wait_ge(s_ph, NT_ALL * l)
                    load_a(l, 1, 1)
                    sp.wait_ge(s_pv, NT_ALL * l)
                    sp.dma_start(ctx_or_pt[:], ctx_d).then_inc(s_ctx, 16)
                else:
                    load_a(l, 0, 0)
                    load_a(l, 1, 1)
                load_b(l, 0, 0, False)
                load_a(l, 2, 0)
                load_b(l, 1, 1, False)
                sp.wait_ge(s_acc0, l + 1)
                sp.dma_start(crow[0:1, :], rows_d[l:l + 1, :]).then_inc(s_row, 16)
                load_a(l, 3, 1)
                with sp.Fori(1, H // 2) as r:
                    for j in range(2):
                        load_b(l, 2 * r + j, j, False)
                        load_a(l, 2 * r + j + 2, j)
                if l == 0:
                    load_x(0)
                for u in (H, H + 1):
                    load_b(l, u, u % 2, False)
                    load_a(l, u + 2, u % 2)
                with sp.Fori(H // 2 + 1, H - 1) as r:
                    for j in range(2):
                        load_b(l, 2 * r + j, j, True)
                        load_a(l, 2 * r + j + 2, j)
                for u in (2 * H - 2, 2 * H - 1):
                    load_b(l, u, u % 2, True)
                if l == 0:
                    for b in range(1, B):
                        load_x(b)
            part = WB * BLK
            sp.wait_ge(s_L, NT_ALL * LAYERS - TPB)
            for n in range(WPARTS):
                at = SPARE * BLK + n * part
                sp.dma_start(store[:, at:at + part], w12_d[:, n * part:(n + 1) * part]).then_inc(s_w1[n], 16)
            sp.wait_ge(s_pv, NT_ALL * LAYERS - TPB)
            for n in range(WPARTS):
                at = (W2_AT + SPARE) * BLK + n * part
                src = w12_d[:, FC * BLK + n * part:FC * BLK + (n + 1) * part]
                sp.dma_start(store[:, at:at + part], src).then_inc(s_w2[n], 16)
            sp.wait_ge(s_xc, NT_ALL * LAYERS)
            sp.dma_start(crow[:], rows_d[LAYERS:LAYERS + 1, :].to_broadcast([P, D])).then_inc(s_row, 16)
            with sp.Fori(0, NT_ALL) as i:
                sp.wait_ge(s_y, i + 1)
                alone(sp, s_passed[2])
                sp.dma_start(y_v[:, bass.ds(i, 1), :].squeeze(1), x[:, bass.ds(i, 1), :].squeeze(1)).then_inc(s_out, 16)
            sp.wait_ge(s_out, 16 * NT_ALL)

        @block.gpsimd
        def _(pool):
            g = nc.gpsimd
            g.memset(neg_half[:], -0.5)
            g.memset(ones[:], 1.0)
            g.memset(ident[:], 0.0).then_inc(s_ident0, 1)
            pool.wait_ge(s_ident0, 1)
            g.affine_select(out=ident[:], in_=ident[:], compare_op=ALU.not_equal, fill=1.0, base=0,
                            pattern=[[-1, P]], channel_multiplier=1).then_inc(s_ident0, 1)
            pool.wait_ge(s_ident0, 2)
            g.tensor_scalar(ident16[:], ident[:], 1.0, 1.0, ALU.mult, ALU.mult).then_inc(s_const, 1)

            def all_max(count, cols):
                pool.wait_ge(s_lm, count)
                g.partition_all_reduce(gm[:, 0:cols], lm[:, 0:cols], P, RMAX).then_inc(s_gm, 1)

            def split_hi(count, slot, col):
                wait_past(pool, s_lo, count - 1)
                hi, src = halves[:, bass.ds(slot * 2 * BLK, BLK)], store[:, bass.ds((slot + SPARE) * BLK, BLK)]
                if isinstance(slot, int):
                    g.tensor_scalar(hi, src, up[:, col:col + 1], 1.0, ALU.mult, ALU.mult).then_inc(s_hi, 1)
                else:
                    alone(pool, s_passed[0])
                    g.tensor_tensor(hi, src, up[:, col:col + 1].to_broadcast([P, BLK]), ALU.mult).then_inc(s_hi, 1)

            def rstd_of(n):
                pool.wait_ge(s_mv, n + 1)
                alone(pool, s_passed[0])
                g.tensor_scalar(ve[:], mv[:, 1:2], EPS, 1.0, ALU.add, ALU.mult).then_inc(s_ve, 1)
                pool.wait_ge(s_ve, n + 1)
                g.tensor_tensor(rstd[:], ve[:], neg_half[:], ALU.pow).then_inc(s_rstd, 1)

            def split_h(n, hi, lo, moves=False):
                pool.wait_ge(s_h32, n + 1)
                alone(pool, s_passed[0])
                src = xh[:].rearrange("p (c q) -> p c q", c=C)
                if moves:
                    g.tensor_tensor(hi, src, ones[:].unsqueeze(1).to_broadcast([P, C, P]), ALU.mult).then_inc(s_hhi, 1)
                else:
                    g.tensor_scalar(hi, src, 1.0, 1.0, ALU.mult, ALU.mult).then_inc(s_hhi, 1)
                pool.wait_ge(s_hhi, n + 1)
                alone(pool, s_passed[0])
                g.tensor_tensor(lo, src, hi, ALU.subtract).then_inc(s_h, 1)

            def add_crow(n, tile, ready):
                pool.wait_ge(s_xh, n + 1)
                if ready > LAYERS:
                    pool.wait_ge(s_row, 16 * ready)
                else:
                    pool.wait_ge(s_crow_ok, ready)
                alone(pool, s_passed[0])
                rows = x[:, bass.ds(tile, 1), :].squeeze(1)
                g.tensor_tensor(rows, rows, crow[:], ALU.add).then_inc(s_xc, 1)

            def mlp_rstd(b, q):
                rstd_of(NT_ALL * LAYERS + TPB * b + q)

            def mlp_rows(b, q):
                split_h(NT_ALL * LAYERS + TPB * b + q, mlp_dst(b, 0, q), mlp_dst(b, 1, q), not isinstance(b, int))

            def mlp_crow(b, q):
                add_crow(NT_ALL * LAYERS + TPB * b + q, TPB * b + q, LAYERS + 1)

            def mlp_split(k):
                landed, slot, col = mlp_block(k)
                pool.wait_ge(landed, 16)
                split_hi(split_base(LAYERS, 0) + k, slot, col)

            for l in range(LAYERS):
                base = NT_ALL * l
                wait_past(pool, s_xc, NT_ALL * l)
                g.memset(crow[:], 0.0).then_inc(s_acc0, 1)
                if l == 0:
                    all_max(1, 6)
                all_max(2 + 2 * l, 4)
                if l == 0:
                    rstd_of(base)
                pool.wait_ge(s_up, 2 + 2 * l)
                pool.wait_ge(s_prep, prep_use(l, 1, 0))

                def m_hi(r):
                    for k in range(4):
                        split_hi(split_base(l, 0) + 4 * r + k, 4 * r + k, UP_M)

                m_hi(0)
                m_hi(1)
                split_h(base, hT[:, 0, 0], hT[:, 0, 1])
                m_hi(2)
                rstd_of(base + 1)
                m_hi(3)
                split_h(base + 1, hT[:, 1, 0], hT[:, 1, 1])
                with pool.Fori(4, H // 2 - 1) as r:
                    m_hi(r)
                rstd_of(base + 2)
                m_hi(H // 2 - 1)
                all_max(3 + 2 * l, 2)
                pool.wait_ge(s_up, 3 + 2 * l)
                pool.wait_ge(s_prep, prep_use(l + 1, 0, 0))

                def vw_hi(first, last):
                    for k in range(first, last):
                        split_hi(split_base(l, 0) + MB + k, MB + k, UP_VW)

                def tile_rows(r, k):
                    n = base + 4 * r + k
                    wait_past(pool, s_L, n - 1)
                    split_h(n, hT[:, k % 2, 0], hT[:, k % 2, 1])

                def tile_crow(r, k):
                    add_crow(base + 4 * r + k, 4 * r + k, l + 1)

                def tile_probs(r, k):
                    pool.wait_ge(s_rc, base + 4 * r + k + 1)
                    v = ls[k % 2].rearrange("p (h s) -> p h s", h=H)
                    g.tensor_tensor(v, v, tot[:, k % 2, :].unsqueeze(2).to_broadcast([P, H, S]),
                                    ALU.mult).then_inc(s_prob, 1)

                def pool_step(r, t):
                    for k in vw_blocks(t):
                        split_hi(split_base(l, 1) + J * (r + 1) + k, MB + J * (r + 1) + k, UP_VW)
                    if t + 2 < NT_ALL:
                        tile_rows(r, t + 2)
                        tile_crow(r, t + 2)
                    if t + 1 < NT_ALL:
                        rstd_of(base + 4 * r + t + 3)
                        tile_probs(r, t + 1)

                vw_hi(0, J // 2)
                tile_rows(0, 2)
                rstd_of(base + 3)
                vw_hi(J // 2, J - 2)
                tile_probs(0, 0)
                tile_rows(0, 3)
                vw_hi(J - 2, J)
                tile_crow(0, 0)
                tile_crow(0, 1)
                tile_probs(0, 1)
                tile_crow(0, 2)
                tile_crow(0, 3)
                rstd_of(base + 4)
                tile_probs(0, 2)
                with pool.Fori(0, LOOP_STEPS // 4) as r:
                    for j in range(4):
                        pool_step(r, LOOP_T0 + j)
                if l < LAYERS - 1:
                    tile_probs(0, NT_ALL - 1)
                else:
                    mlp_rows(0, 0)
                    mlp_rstd(0, 1)
                    mlp_crow(0, 0)
                    mlp_rows(0, 1)
                    mlp_crow(0, 1)
                    mlp_rstd(0, 2)
                    tile_probs(0, NT_ALL - 1)
                    mlp_rstd(0, 3)
                    mlp_rows(0, 2)
                    mlp_split(0)
                    mlp_split(1)
                    mlp_crow(0, 2)
                    mlp_split(2)
                    mlp_split(3)
                    mlp_rows(0, 3)
                    mlp_crow(0, 3)
                    for k in range(4, 2 * MLP_AHEAD):
                        mlp_split(k)

            def pool_batch(b, more):
                for f in range(FC):
                    n = FC * b + f
                    if more and f % 4 == 0:
                        mlp_rstd(b + 1, f // 4)
                    wait_past(pool, s_fc2, n - 1)
                    pool.wait_ge(s_gelu, n + 1)
                    alone(pool, s_passed[0])
                    g.tensor_scalar(gh[:, f % 2, 0], g32[:, f % 2], up[:, UP_G:UP_G + 1], 1.0,
                                    ALU.mult, ALU.mult).then_inc(s_ghi, 1)
                    if isinstance(b, int) and b == 0:
                        for k in late_blocks(f):
                            mlp_split(k)
                    if more and f % 4 == 2:
                        mlp_rows(b + 1, f // 4)
                    if more and f % 4 == 3:
                        mlp_crow(b + 1, f // 4)

            pool_batch(0, True)
            with pool.Fori(1, B - 1) as b:
                pool_batch(b, True)
            pool_batch(B - 1, False)

        @block.scalar
        def _(act):
            a = nc.scalar
            act.wait_ge(s_vec, 16)
            act.wait_ge(s_up, 1)

            def head_kv(l, phase, h, slot):
                u = prep_use(l, phase, h)
                act.wait_ge(s_kv_mm, u + 1)
                wait_past(act, s_prep_mm, u - 1)
                wait_past(act, s_mag, u - 1)
                if phase == 0:
                    o = l * V_LAYER + V_BQ
                    a.activation(bq_now[:, slot:slot + 1], col(vec[:, o:o + H], h), ACT.Copy)
                a.activation(kv[:, slot], ptp[:, slot * BLK:slot * BLK + BS], ACT.Identity,
                             bias=col(kvb[:, l, phase], h)).then_inc(s_kv, 1)

            def col(v, h):
                return v[:, bass.ds(h, 1)]

            def head_m(l, h, slot):
                n = H * l + h
                act.wait_ge(s_qkb_mm, n + 1)
                a.activation(qk_bias[:].rearrange("p (b n) -> p b n", b=B)[:, :, bass.ds(h * S, S)],
                             acc[:, 0:BS].rearrange("p (b s) -> p b s", b=B), ACT.Copy,
                             scale=QK_SCALE).then_inc(s_qkb, 1)
                act.wait_ge(s_prep_mm, prep_use(l, 0, h) + 1)
                a.activation(m_out[:, :, :, bass.ds(h * S, S)],
                             pairs[slot][:].rearrange("p (c b s) -> p c b s", c=C, b=B),
                             ACT.Copy).then_inc(s_prep, 1)

            def head_vw(l, h, hh, slot):
                act.wait_ge(s_prep_mm, prep_use(l, 1, h) + 1)
                for par in range(2):
                    src = pairs[slot][S * par:S * (par + 1), :].rearrange("p (g n) -> p g n", g=2)
                    last = a.activation(vw_out[S * slot:S * (slot + 1), par::2, hh, :], src, ACT.Copy)
                last.then_inc(s_prep, 1)

            def affine(n, vector):
                act.wait_ge(s_nt, n + 1)
                for c in range(C):
                    last = a.activation(xh[:, c * P:(c + 1) * P], ntp[:, c * P:(c + 1) * P], ACT.Identity,
                                        scale=lnv[:, vector, c:c + 1], bias=lnv[:, vector, C + c:C + c + 1])
                last.then_inc(s_h32, 1)

            def look_at(l, n):
                wait_past(act, s_wm, 16 * (H // 2 * l + n))
                at = (SPARE + MB) * BLK + n * LOOK
                src = w12_d[:, bass.ds(l * FC * D + n * LOOK, LOOK)]
                act.dma_start(store[:, bass.ds(at, LOOK)], src).then_inc(s_wm, 16)

            for l in range(LAYERS):
                base = NT_ALL * l
                head_kv(l, 0, 0, 0)
                for h in range(2):
                    head_kv(l, 0, h + 1, (h + 1) % 2)
                    head_m(l, h, h % 2)
                look_at(l, 0)
                with act.Fori(1, H // 2 - 1) as r:
                    for j in range(2):
                        head_kv(l, 0, 2 * r + j + 1, (j + 1) % 2)
                        head_m(l, 2 * r + j, j)
                    look_at(l, r)
                head_kv(l, 0, H - 1, 1)
                head_m(l, H - 2, 0)
                look_at(l, H // 2 - 1)
                head_kv(l, 1, 0, 0)
                head_m(l, H - 1, 1)
                act.wait_ge(s_wm_mag, H // 2 * (l + 1))

                def two_heads(r):
                    for j in range(2):
                        head_kv(l, 1, 2 * r + j + 1, (j + 1) % 2)
                        head_vw(l, 2 * r + j, r, j)

                for r in range(4):
                    two_heads(r)
                    if r % 2:
                        affine(base + r // 2, l)
                with act.Fori(4, H // 2 - 1) as r:
                    two_heads(r)
                head_kv(l, 1, H - 1, 1)
                head_vw(l, H - 2, H // 2 - 1, 0)
                head_vw(l, H - 1, H // 2 - 1, 1)
                act.wait_ge(s_crow_mm, l + 1)
                a.activation(crow[:], acc[:], ACT.Copy).then_inc(s_crow_ok, 1)

                def tile_exp(r, k):
                    n = base + 4 * r + k
                    act.wait_ge(s_top, n + 1)
                    a.activation(etop[:, k % 2], top[:, k % 2], ACT.Exp, scale=-1.0).then_inc(s_etop, 1)
                    act.wait_ge(s_sub, n + 1)
                    a.activation(ls[k % 2], ls[k % 2], ACT.Exp).then_inc(s_exp, 1)

                def probs_hi(r, k):
                    n = base + 4 * r + k
                    act.wait_ge(s_prob, n + 1)
                    wait_past(act, s_tp, 2 * n)
                    a.activation(ph[:, 0], ls[k % 2], ACT.Copy).then_inc(s_phi, 1)

                def probs_t(r, k):
                    n = base + 4 * r + k
                    wait_past(act, s_pv, n)
                    for half in range(2):
                        act.wait_ge(s_tp, 2 * n + half + 1)
                        a.activation(pt[:, half], ptp16[:, half, 0:HS], ACT.Copy).then_inc(s_pt, 1)

                def act_step(r, t):
                    if t < NT_ALL:
                        probs_hi(r, t)
                    probs_t(r, t - 1)
                    if t + 2 < NT_ALL:
                        affine(base + 4 * r + t + 2, l)
                    if t + 1 < NT_ALL:
                        tile_exp(r, t + 1)

                affine(base + 2, l)
                tile_exp(0, 0)
                affine(base + 3, l)
                probs_hi(0, 0)
                tile_exp(0, 1)
                probs_t(0, 0)
                probs_hi(0, 1)
                tile_exp(0, 2)
                with act.Fori(0, LOOP_STEPS // 4) as r:
                    for j in range(4):
                        act_step(r, LOOP_T0 + j)
                def mlp_affine(q):
                    if l == LAYERS - 1:
                        affine(NT_ALL * LAYERS + q, LAYERS)

                probs_hi(0, 14)
                mlp_affine(0)
                probs_t(0, 13)
                mlp_affine(1)
                tile_exp(0, 15)
                probs_t(0, 14)
                mlp_affine(2)
                probs_hi(0, 15)
                probs_t(0, 15)
                mlp_affine(3)

            base = NT_ALL * LAYERS

            def act_batch(b, more):
                for f in range(FC):
                    n = FC * b + f
                    if more and f % 4 == 2:
                        affine(base + TPB * (b + 1) + f // 4, LAYERS)
                    act.wait_ge(s_fc1, n + 1)
                    wait_past(act, s_g, n - 1)
                    o = V_MLP + 2 * C + f
                    a.activation(g32[:, f % 2], ptp[:, (f % 2) * BLK:(f % 2 + 1) * BLK], ACT.Gelu,
                                 scale=dn[:, DN_F1:DN_F1 + 1], bias=vec[:, o:o + 1]).then_inc(s_gelu, 1)

            act_batch(0, True)
            with act.Fori(1, B - 1) as b:
                act_batch(b, True)
            act_batch(B - 1, False)

        @block.vector
        def _(dve):
            v = nc.vector
            chained = [0]

            def link(instruction):
                chained[0] += 1
                instruction.then_inc(s_dve, 1)
                dve.wait_ge(s_dve, chained[0])

            def power(src, at, n=1):
                p_ap = dn[:, at:at + n]
                link(v.tensor_scalar(p_ap.bitcast(U32), src.bitcast(U32), EXP_MASK, None, ALU.bitwise_and))
                link(v.tensor_scalar(p_ap, p_ap, 2.0 ** -80, None, ALU.max))
                link(v.reciprocal(up[:, at:at + n], p_ap))
                link(v.tensor_scalar(up[:, at:at + n], up[:, at:at + n], TOP, None, ALU.mult))
                return v.tensor_scalar(p_ap, p_ap, 1.0 / TOP, None, ALU.mult)

            dve.wait_ge(s_vec, 16)
            for l in range(LAYERS):
                o = l * V_LAYER
                v.tensor_tensor(kvb[:, l], vec[:, o + V_BK:o + V_BK + 2 * H].rearrange("p (a h) -> p a h", a=2),
                                vec[:, o + V_BIASK:o + V_BIASK + 2 * H].rearrange("p (a h) -> p a h", a=2),
                                ALU.subtract)
            ln_at = [V_LNS, V_LAYER + V_LNS, V_MLP]
            for n, o in enumerate(ln_at):
                last = v.tensor_reduce(lm[:, 2 * n:2 * n + 2], vec[:, o:o + 2 * C].rearrange("p (a c) -> p a c", a=2),
                                       AX.X, ALU.max, apply_absolute_value=True)
            last.then_inc(s_lm, 1)
            dve.wait_ge(s_gm, 1)
            for n in range(LAYERS + 1):
                last = v.scalar_tensor_tensor(bound[:, n:n + 1], gm[:, 2 * n:2 * n + 1], LN_MAX,
                                              gm[:, 2 * n + 1:2 * n + 2], ALU.mult, ALU.add)
            link(last)
            link(power(bound[:, 0:3], UP_LN, 3))
            for n, o in enumerate(ln_at):
                last = v.tensor_scalar(lnv[:, n], vec[:, o:o + 2 * C], up[:, UP_LN + n:UP_LN + n + 1], None, ALU.mult)
            last.then_inc(s_up, 1)

            def split_lo(count, slot, col):
                dve.wait_ge(s_hi, count + 1)
                v.scalar_tensor_tensor(halves[:, bass.ds(slot * 2 * BLK + BLK, BLK)],
                                       store[:, bass.ds((slot + SPARE) * BLK, BLK)], up[:, col:col + 1],
                                       halves[:, bass.ds(slot * 2 * BLK, BLK)],
                                       ALU.mult, ALU.subtract).then_inc(s_lo, 1)

            def mlp_split(k):
                landed, slot, col = mlp_block(k)
                dve.wait_ge(landed, 16)
                split_lo(split_base(LAYERS, 0) + k, slot, col)

            def row_stats(n, tile, loaded=None):
                if loaded is not None:
                    dve.wait_ge(loaded, 16)
                else:
                    dve.wait_ge(s_xr, n - NT_ALL + 1)
                v.bn_stats(stats[:], x[:, bass.ds(tile, 1), :].squeeze(1)).then_inc(s_bn, 1)
                dve.wait_ge(s_bn, n + 1)
                alone(dve, s_passed[1])
                v.bn_aggr(mv[:], stats[:]).then_inc(s_mv, 1)

            def norm_rows(n, tile):
                dve.wait_ge(s_rstd, n + 1)
                wait_past(dve, s_h, n)
                v.tensor_scalar(xh[:], x[:, bass.ds(tile, 1), :].squeeze(1), mv[:, 0:1], rstd[:, 0:1], ALU.subtract,
                                ALU.mult).then_inc(s_xh, 1)

            def look_at(l, n):
                dve.wait_ge(s_wm, 16 * (H // 2 * l + n + 1))
                v.tensor_reduce(mw[:, bass.ds(n, 1)], store[:, bass.ds((SPARE + MB) * BLK + n * LOOK, LOOK)],
                                AX.X, ALU.max, apply_absolute_value=True).then_inc(s_wm_mag, 1)

            def head_mag(l, phase, r, j):
                dve.wait_ge(s_ring_b[j], 16 * (H * l + H // 2 * phase + r + 1))
                v.tensor_reduce(mx[:, 0, bass.ds(2 * r + j, 1)], ring[j][:, D:2 * D], AX.X, ALU.max,
                                apply_absolute_value=True)
                dve.wait_ge(s_kv, prep_use(l, phase, 2 * r + j) + 1)
                v.tensor_reduce(mx[:, 1, bass.ds(2 * r + j, 1)], kv[:, j], AX.X, ALU.max,
                                apply_absolute_value=True).then_inc(s_mag, 1)

            def all_heads_mag(l, phase):
                dve.wait_ge(s_mag, prep_use(l, phase + 1, 0))
                v.tensor_reduce(lm[:, 0:2], mx[:], AX.X, ALU.max).then_inc(s_lm, 1)

            def product_scale(at):
                link(v.tensor_scalar(bound[:, 3:4], gm[:, 0:1], gm[:, 1:2], float(K), ALU.mult, ALU.mult))
                link(power(bound[:, 3:4], at))

            for l in range(LAYERS):
                base = NT_ALL * l
                for j in range(2):
                    head_mag(l, 0, 0, j)
                with dve.Fori(1, H // 2) as r:
                    for j in range(2):
                        head_mag(l, 0, r, j)
                    look_at(l, r - 1)
                look_at(l, H // 2 - 1)
                dve.wait_ge(s_wm_mag, H // 2 * (l + 1))
                v.tensor_reduce(lm[:, 2:3], mw[:], AX.X, ALU.max)
                v.tensor_reduce(lm[:, 3:4], vec[:, V_MLP + 2 * C:V_ALL], AX.X, ALU.max, apply_absolute_value=True)
                all_heads_mag(l, 0)
                if l == 0:
                    row_stats(base, 0, s_x[0])
                dve.wait_ge(s_gm, 2 + 2 * l)
                product_scale(UP_M)
                link(v.tensor_scalar(dn[:, DN_L:DN_L + 1], dn[:, UP_M:UP_M + 1], dn[:, UP_LN + l:UP_LN + l + 1],
                                     QK_SCALE, ALU.mult, ALU.mult))
                v.tensor_scalar(dn[:, DN_L:DN_L + 1], dn[:, DN_L:DN_L + 1], 1.0, None,
                                ALU.mult).then_inc(s_up, 1)
                dve.wait_ge(s_row, 16 * (l + 1))

                def add_bias_v(r, j):
                    wait_past(dve, s_crow, H * l + 2 * r + j)
                    o = l * V_LAYER + V_BIASV
                    v.scalar_tensor_tensor(crow[:], ring[j][:, D:2 * D], vec[:, bass.ds(2 * r + (o + j), 1)],
                                           crow[:], ALU.mult, ALU.add).then_inc(s_crow, 1)

                def m_lo(first, count):
                    for k in range(count):
                        split_lo(split_base(l, 0) + first + k, first + k, UP_M)

                def v_heads(r):
                    for j in range(2):
                        head_mag(l, 1, r, j)
                        add_bias_v(r, j)
                        m_lo(4 * r + 2 * j, 2)

                v_heads(0)
                norm_rows(base, 0)
                v_heads(1)
                v_heads(2)
                row_stats(base + 1, 1, s_x[0] if l == 0 else None)
                if l:
                    link(power(gm[:, 2:3], UP_W2))
                    link(v.tensor_tensor(dn[:, DN_F2:DN_F2 + 1], dn[:, UP_W2:UP_W2 + 1], dn[:, UP_G:UP_G + 1],
                                         ALU.mult))
                norm_rows(base + 1, 1)
                v_heads(3)
                with dve.Fori(4, H // 2 - 1) as r:
                    v_heads(r)
                row_stats(base + 2, 2, s_x[0] if l == 0 else None)
                for j in range(2):
                    head_mag(l, 1, H // 2 - 1, j)
                    add_bias_v(H // 2 - 1, j)
                all_heads_mag(l, 1)
                norm_rows(base + 2, 2)
                m_lo(MB - 4, 4)
                row_stats(base + 3, 3, s_x[0] if l == 0 else None)
                dve.wait_ge(s_gm, 3 + 2 * l)
                product_scale(UP_VW)
                v.tensor_scalar(dn[:, DN_VW:DN_VW + 1], dn[:, UP_VW:UP_VW + 1], 1.0 / TOP, None,
                                ALU.mult).then_inc(s_up, 1)
                if l == 0:
                    for b in range(1, B):
                        dve.wait_ge(s_x[b], 16)

                def first_vw_lo(first, last):
                    for k in range(first, last):
                        split_lo(split_base(l, 0) + MB + k, MB + k, UP_VW)

                def tile_less_top(r, k):
                    n = base + 4 * r + k
                    slot = k % 2
                    heads = ls[slot].rearrange("p (h s) -> p h s", h=H)
                    tops = top[:, slot].unsqueeze(2).to_broadcast([P, H, S])
                    b = r + k // 4
                    dve.wait_ge(s_L, n + 1)
                    dve.wait_ge(s_qkb, H * (l + 1))
                    v.scalar_tensor_tensor(ls[slot], pairs[slot][:], dn[:, DN_L:DN_L + 1],
                                           qk_bias[:, bass.ds(b * HS, HS)], ALU.mult, ALU.add).then_inc(s_ls, 1)
                    dve.wait_ge(s_ls, n + 1)
                    v.tensor_reduce(top[:, slot], heads, AX.X, ALU.max).then_inc(s_top0, 1)
                    dve.wait_ge(s_top0, n + 1)
                    v.tensor_scalar(top[:, slot], top[:, slot], 0.0, None, ALU.max).then_inc(s_top, 1)
                    dve.wait_ge(s_top, n + 1)
                    v.tensor_tensor(heads, heads, tops, ALU.subtract).then_inc(s_sub, 1)

                def tile_sums(r, k):
                    n = base + 4 * r + k
                    slot = k % 2
                    dve.wait_ge(s_exp, n + 1)
                    v.tensor_reduce(tot[:, slot], ls[slot].rearrange("p (h s) -> p h s", h=H), AX.X,
                                    ALU.add).then_inc(s_sum, 1)
                    dve.wait_ge(s_sum, n + 1)
                    dve.wait_ge(s_etop, n + 1)
                    v.tensor_tensor(tot[:, slot], tot[:, slot], etop[:, slot], ALU.add).then_inc(s_tot, 1)
                    dve.wait_ge(s_tot, n + 1)
                    v.tensor_scalar(tot[:, slot], tot[:, slot], 1.0 / TOP, None, ALU.mult).then_inc(s_tot2, 1)
                    dve.wait_ge(s_tot2, n + 1)
                    v.reciprocal(tot[:, slot], tot[:, slot]).then_inc(s_rc, 1)

                def probs_lo(r, k):
                    n = base + 4 * r + k
                    dve.wait_ge(s_phi, n + 1)
                    v.tensor_tensor(ph[:, 1], ls[k % 2], ph[:, 0], ALU.subtract).then_inc(s_ph, 1)

                def tile_out(r, k):
                    m = base + 4 * r + k
                    x_tile = x[:, bass.ds(4 * r + k, 1), :].squeeze(1)
                    dve.wait_ge(s_pv, m + 1)
                    dve.wait_ge(s_xc, m + 1)
                    v.scalar_tensor_tensor(x_tile, acc[:], dn[:, DN_VW:DN_VW + 1], x_tile,
                                           ALU.mult, ALU.add).then_inc(s_xr, 1)

                def next_stats(r, k):
                    if k < NT_ALL:
                        row_stats(base + 4 * r + k, (4 * r + k) % NT_ALL, s_x[0] if l == 0 else None)

                def vw_lo(r, t):
                    for k in vw_blocks(t):
                        split_lo(split_base(l, 1) + J * (r + 1) + k, MB + J * (r + 1) + k, UP_VW)

                def dve_step(r, t):
                    if t + 2 < NT_ALL:
                        norm_rows(base + 4 * r + t + 2, 4 * r + t + 2)
                    if t < NT_ALL:
                        probs_lo(r, t)
                    if t == 5:
                        vw_lo(r, t)
                    if t + 1 < NT_ALL:
                        tile_less_top(r, t + 1)
                        next_stats(r, t + 3)
                        tile_sums(r, t + 1)
                    tile_out(r, t - 1)
                    if t != 5:
                        vw_lo(r, t)

                first_vw_lo(0, J // 2)
                tile_less_top(0, 0)
                norm_rows(base + 3, 3)
                tile_sums(0, 0)
                tile_less_top(0, 1)
                probs_lo(0, 0)
                first_vw_lo(J // 2, J - 2)
                tile_sums(0, 1)
                first_vw_lo(J - 2, J)
                tile_less_top(0, 2)
                probs_lo(0, 1)
                next_stats(0, 4)
                tile_sums(0, 2)
                tile_out(0, 0)
                with dve.Fori(0, LOOP_STEPS // 4) as r:
                    for j in range(4):
                        dve_step(r, LOOP_T0 + j)
                if l == 0:
                    link(power(gm[:, 2:3], UP_W1))
                    link(v.tensor_scalar(bound[:, 3:4], gm[:, 2:3], bound[:, 2:3], float(D), ALU.mult, ALU.mult))
                    link(v.tensor_tensor(bound[:, 3:4], bound[:, 3:4], gm[:, 3:4], ALU.add))
                    link(power(bound[:, 3:4], UP_G))
                    link(v.tensor_tensor(dn[:, DN_F1:DN_F1 + 1], dn[:, UP_W1:UP_W1 + 1],
                                         dn[:, UP_LN + LAYERS:UP_LN + LAYERS + 1], ALU.mult))
                    probs_lo(0, 14)
                    tile_less_top(0, 15)
                    tile_sums(0, 15)
                    tile_out(0, 13)
                    probs_lo(0, 15)
                    tile_out(0, 14)
                    tile_out(0, 15)
                else:
                    def mlp_stats(q):
                        row_stats(NT_ALL * LAYERS + q, q)

                    def mlp_norm(q):
                        norm_rows(NT_ALL * LAYERS + q, q)

                    mlp_norm(0)
                    probs_lo(0, 14)
                    mlp_stats(1)
                    mlp_norm(1)
                    tile_less_top(0, 15)
                    mlp_stats(2)
                    tile_sums(0, 15)
                    tile_out(0, 13)
                    mlp_norm(2)
                    mlp_stats(3)
                    probs_lo(0, 15)
                    mlp_norm(3)
                    mlp_split(0)
                    mlp_split(1)
                    tile_out(0, 14)
                    for k in range(2, 2 * MLP_AHEAD):
                        mlp_split(k)
                    tile_out(0, 15)

            base = NT_ALL * LAYERS

            def dve_batch(b, more):
                for f in range(FC):
                    n = FC * b + f
                    row = (base + TPB * (b + 1) + f // 4, TPB * (b + 1) + f // 4)
                    if more and f % 4 == 0:
                        row_stats(*row)
                    dve.wait_ge(s_ghi, n + 1)
                    v.scalar_tensor_tensor(gh[:, f % 2, 1], g32[:, f % 2], up[:, UP_G:UP_G + 1], gh[:, f % 2, 0],
                                           ALU.mult, ALU.subtract).then_inc(s_g, 1)
                    if isinstance(b, int) and b == 0:
                        for k in late_blocks(f):
                            mlp_split(k)
                    if more and f % 4 == 0:
                        norm_rows(*row)
                for q in range(TPB):
                    i = TPB * b + q
                    if q < TPB - 1:
                        dve.wait_ge(s_fc2_tile, (TPB - 1) * b + q + 1)
                    else:
                        dve.wait_ge(s_fc2, FC * (b + 1))
                    dve.wait_ge(s_xc, base + i + 1)
                    x_tile = x[:, bass.ds(i, 1), :].squeeze(1)
                    v.scalar_tensor_tensor(x_tile, pairs[q // 2][:, (q % 2) * BLK:(q % 2 + 1) * BLK],
                                           dn[:, DN_F2:DN_F2 + 1], x_tile, ALU.mult, ALU.add).then_inc(s_y, 1)

            dve_batch(0, True)
            with dve.Fori(1, B - 1) as b:
                dve_batch(b, True)
            dve_batch(B - 1, False)

        @block.tensor
        def _(pe):
            t_ = nc.tensor

            def head_kv(l, phase, h, slot, slot_uses):
                u = prep_use(l, phase, h)
                pe.wait_ge(s_ring_a[slot], 16 * slot_uses)
                wait_past(pe, s_kv, u - 1)
                for c in range(C):
                    last = t_.matmul(ptp[:, slot * BLK:slot * BLK + BS], ring[slot][:, c * P:(c + 1) * P],
                                     cT(l, phase)[:, c, :], start=(c == 0), stop=(c == C - 1))
                last.then_inc(s_kv_mm, 1)

            def head_m(l, h, slot, slot_uses):
                u = prep_use(l, 0, h)
                pe.wait_ge(s_kv, u + 1)
                wait_past(pe, s_qkb, H * l + h)
                if isinstance(h, int) and h == 0:
                    wait_past(pe, s_xr, NT_ALL * l)
                t_.matmul(acc[:, 0:BS], bq_now[:, slot:slot + 1].to_broadcast([P, P]), kv[:, slot],
                          start=True, stop=True).then_inc(s_qkb_mm, 1)
                wait_past(pe, s_prep, u - 1)
                pe.wait_ge(s_ring_b[slot], 16 * slot_uses)
                for c in range(C):
                    last = t_.matmul(pairs[slot][:, c * BS:(c + 1) * BS], ring[slot][:, D + c * P:D + (c + 1) * P],
                                     kv[:, slot], start=True, stop=True)
                last.then_inc(s_prep_mm, 1)

            def head_vw(l, h, slot, slot_uses):
                u = prep_use(l, 1, h)
                pe.wait_ge(s_kv, u + 1)
                pe.wait_ge(s_prep, u - 1)
                pe.wait_ge(s_ring_b[slot], 16 * slot_uses)
                for g in range(2):
                    last = t_.matmul(pairs[slot][:, g * BLK:(g + 1) * BLK], kv[:, slot, g * P:(g + 1) * P],
                                     ring[slot][:, D:2 * D], start=True, stop=True)
                last.then_inc(s_prep_mm, 1)

            def transposes(n):
                pe.wait_ge(s_xh, n + 1)
                wait_past(pe, s_h32, n)
                for c in range(C):
                    last = t_.transpose(ntp[:, c * P:(c + 1) * P], xh[:, c * P:(c + 1) * P], ident[:])
                last.then_inc(s_nt, 1)

            pe.wait_ge(s_const, 1)
            for l in range(LAYERS):
                base = NT_ALL * l
                uses = H * l
                pe.wait_ge(s_ctx, 16 * (2 * l if l else 1))
                head_kv(l, 0, 0, 0, uses + 1)
                for h in range(2):
                    head_kv(l, 0, h + 1, (h + 1) % 2, uses + (h + 1) // 2 + 1)
                    head_m(l, h, h % 2, uses + 1)
                with pe.Fori(1, H // 2 - 1) as r:
                    for j in range(2):
                        head_kv(l, 0, 2 * r + j + 1, (j + 1) % 2, uses + r + (j + 1) // 2 + 1)
                        head_m(l, 2 * r + j, j, uses + r + 1)
                head_kv(l, 0, H - 1, 1, uses + H // 2)
                head_m(l, H - 2, 0, uses + H // 2)
                if l:
                    pe.wait_ge(s_ctx, 16 * (2 * l + 1))
                head_kv(l, 1, 0, 0, uses + H // 2 + 1)
                head_m(l, H - 1, 1, uses + H // 2)
                def two_heads(r):
                    for j in range(2):
                        head_kv(l, 1, 2 * r + j + 1, (j + 1) % 2, uses + H // 2 + r + (j + 1) // 2 + 1)
                        head_vw(l, 2 * r + j, j, uses + H // 2 + r + 1)

                for r in range(4):
                    two_heads(r)
                    if r % 2:
                        transposes(base + r // 2)
                with pe.Fori(4, H // 2 - 1) as r:
                    two_heads(r)
                head_kv(l, 1, H - 1, 1, uses + H)
                head_vw(l, H - 2, 0, uses + H)
                head_vw(l, H - 1, 1, uses + H)
                pe.wait_ge(s_crow, H * (l + 1))
                pe.wait_ge(s_qkb, H * (l + 1))
                t_.matmul(acc[:], ones[:], crow[:], start=True, stop=True).then_inc(s_crow_mm, 1)

                def probs_transposes(r, k):
                    n = base + 4 * r + k
                    pe.wait_ge(s_ph, n + 1)
                    wait_past(pe, s_pt, 2 * n)
                    for half in range(2):
                        for j in range(J):
                            last = t_.transpose(ptp16[:, half, j * P:(j + 1) * P], ph[:, half, j * P:(j + 1) * P],
                                                ident16[:])
                        last.then_inc(s_tp, 1)

                def logits(r, k, chunks=range(C)):
                    n = base + 4 * r + k
                    slot = k % 2
                    b = r + k // 4
                    pe.wait_ge(s_h, n + 1)
                    pe.wait_ge(s_lo, split_base(l, 0) + 2 * C * (b + 1))
                    wait_past(pe, s_ls, n - 1)
                    for c in chunks:
                        for half, mhalf in ((0, 0), (0, 1), (1, 0)):
                            for g in range(2):
                                at = (b * 2 * C + 2 * c + g) * 2 * BLK + mhalf * BLK
                                last = t_.matmul(pairs[slot][:, g * BLK:(g + 1) * BLK], hT[:, slot, half, c, :],
                                                 halves[:, bass.ds(at, BLK)], start=(c == 0 and half + mhalf == 0),
                                                 stop=(c == C - 1 and half == 1))
                    if C - 1 in chunks:
                        last.then_inc(s_L, 1)

                def attend(r, k):
                    n = base + 4 * r + k
                    b = r + k // 4
                    pe.wait_ge(s_pt, 2 * n + 1)
                    first = k % TPB == 0
                    if not first:
                        pe.wait_ge(s_lo, split_base(l, 1) + J * (b + 1))
                    pe.wait_ge(s_crow_ok, l + 1)
                    wait_past(pe, s_xr, n)
                    for half, vhalves in ((0, (0, 1)), (1, (0,))):
                        if half:
                            pe.wait_ge(s_pt, 2 * n + 2)
                        for j in range(J):
                            if first and not half:
                                pe.wait_ge(s_lo, split_base(l, 1) + J * b + j + 1)
                            for vhalf in vhalves:
                                at = (MB + b * J + j) * 2 * BLK + vhalf * BLK
                                last = t_.matmul(acc[:], pt[:, half, j * P:(j + 1) * P], halves[:, bass.ds(at, BLK)],
                                                 start=(j == 0 and half + vhalf == 0),
                                                 stop=(j == J - 1 and half == 1))
                    last.then_inc(s_pv, 1)

                def pe_step(r, t):
                    logits(r, t + 1, range(C // 2))
                    probs_transposes(r, t - 1)
                    logits(r, t + 1, range(C // 2, C))
                    if t + 2 < NT_ALL:
                        transposes(base + 4 * r + t + 2)
                    attend(r, t - 1)

                pe.wait_ge(s_prep, prep_use(l + 1, 0, 0) - 1)
                logits(0, 0)
                transposes(base + 2)
                pe.wait_ge(s_prep, prep_use(l + 1, 0, 0))
                logits(0, 1)
                logits(0, 2)
                transposes(base + 3)
                probs_transposes(0, 0)
                attend(0, 0)
                with pe.Fori(0, LOOP_STEPS // 4) as r:
                    for j in range(4):
                        pe_step(r, LOOP_T0 + j)
                def mlp_transposes(q):
                    if l == LAYERS - 1:
                        transposes(NT_ALL * LAYERS + q)

                probs_transposes(0, 13)
                mlp_transposes(0)
                logits(0, 15)
                mlp_transposes(1)
                attend(0, 13)
                probs_transposes(0, 14)
                mlp_transposes(2)
                attend(0, 14)
                probs_transposes(0, 15)
                mlp_transposes(3)
                attend(0, 15)

            base = NT_ALL * LAYERS

            def fc1(b, f):
                n = FC * b + f
                wait_past(pe, s_gelu, n - 1)
                pe.wait_ge(s_lo, split_base(LAYERS, 0) + 2 * f + 1)
                pe.wait_ge(s_h, base + TPB * (b + 1))
                for c in range(C):
                    for whalf, half in ((0, 0), (0, 1), (1, 0)):
                        at = (f * 2 + whalf) * BLK + c * P
                        src = mlp_rows_at(b, half)[:, c, :]
                        last = t_.matmul(ptp[:, (f % 2) * BLK:(f % 2 + 1) * BLK], halves[:, at:at + P], src,
                                         start=(c == 0 and whalf + half == 0), stop=(c == C - 1 and whalf == 1))
                last.then_inc(s_fc1, 1)

            def fc2(b, f):
                n = FC * b + f
                pe.wait_ge(s_g, n + 1)
                pe.wait_ge(s_lo, split_base(LAYERS, 0) + 2 * f + 2)
                for q in range(TPB):
                    if f == 0:
                        wait_past(pe, s_y, TPB * (b - 1) + q + 1)
                    for half, whalf in ((0, 0), (0, 1), (1, 0)):
                        at = ((W2_AT + f) * 2 + whalf) * BLK
                        last = t_.matmul(pairs[q // 2][:, (q % 2) * BLK:(q % 2 + 1) * BLK],
                                         gh[:, f % 2, half, q * P:(q + 1) * P], halves[:, bass.ds(at, BLK)],
                                         start=(f == 0 and half + whalf == 0), stop=(f == FC - 1 and half == 1))
                    if f == FC - 1 and q < TPB - 1:
                        last.then_inc(s_fc2_tile, 1)
                last.then_inc(s_fc2, 1)

            def pe_batch(b, more):
                fc1(b, 0)
                for f in range(FC):
                    if f + 1 < FC:
                        fc1(b, f + 1)
                    if more and f % 4 == 1:
                        transposes(base + TPB * (b + 1) + f // 4)
                    fc2(b, f)

            pe_batch(0, True)
            with pe.Fori(1, B - 1) as b:
                pe_batch(b, True)
            pe_batch(B - 1, False)


def kernel(**inputs):
    import numpy as np
    import concourse.bacc as bacc
    from concourse.bass_utils import run_bass_kernel_spmd

    w = {k.replace("L0_xattn_", ""): np.asarray(v) for k, v in inputs.items()}

    def by_chunk(v):
        return v.reshape(-1, P).T

    def heads_in(m):
        return m.reshape(C, P, H, K).transpose(2, 1, 0, 3).reshape(H, P, C * K)

    weights = np.stack([np.concatenate([
        np.concatenate([heads_in(w[f"wk{i}"]), w[f"wq{i}"].T.reshape(H, K, D)], axis=2),
        np.concatenate([heads_in(w[f"wv{i}"]), w[f"wo{i}"].reshape(H, K, D)], axis=2)]) for i in (1, 2)])
    cols = []
    for i in (1, 2):
        for name in (f"bq{i}", f"bk{i}", f"bv{i}", f"bias_k{i}", f"bias_v{i}", f"ln{i}_scale", f"ln{i}_offset"):
            cols.append(by_chunk(w[name].reshape(-1)))
    for name in ("ln_mlp_scale", "ln_mlp_offset", "b_fc1"):
        cols.append(by_chunk(w[name]))
    arrays = {
        "x": w["x"].reshape(B * Q, D),
        "ctxT": w["ctx_2048"].reshape(BS, C, P).transpose(2, 1, 0).reshape(P, C * BS),
        "weights": weights,
        "vectors": np.concatenate(cols, axis=1),
        "rows": np.stack([w["bo1"], w["bo2"], w["b_fc2"]]),
        "w12": np.concatenate([w["w_fc1"].reshape(C, P, FC, P).transpose(1, 2, 0, 3).reshape(P, FC * D),
                               w["w_fc2"].reshape(FC, P, D).transpose(1, 0, 2).reshape(P, FC * D)], axis=1),
    }
    arrays = {k: np.ascontiguousarray(v) for k, v in arrays.items()}
    nc = bacc.Bacc("TRN2", target_bir_lowering=False, num_devices=1)
    args = [nc.dram_tensor(k + "_dram", v.shape, F32, kind="ExternalInput").ap() for k, v in arrays.items()]
    args.append(nc.dram_tensor("y_dram", (B * Q, D), F32, kind="ExternalOutput").ap())
    program(nc, *args)
    r = run_bass_kernel_spmd(nc, [{k + "_dram": v for k, v in arrays.items()}], core_ids=[0])
    return np.asarray(r.results[0]["y_dram"]).reshape(B, Q, D)
```
